# Optimizing a Trainium2 kernel written in Bass

```python
import numpy as np
import jax
import jax.numpy as jnp

def _softmax(x, axis=-1):
    return jax.nn.softmax(x, axis=axis)

def _gelu(x):
    return jax.nn.gelu(x, approximate=True)

def _silu(x):
    return jax.nn.silu(x)

def _sigmoid(x):
    return jax.nn.sigmoid(x)

def _layernorm(x, axis=-1, eps=1e-05):
    m = jnp.mean(x, axis=axis, keepdims=True)
    v = jnp.var(x, axis=axis, keepdims=True)
    return (x - m) / jnp.sqrt(v + eps)

def _scatter_add(tgt, idx, src, axis=0):
    return tgt.at[idx].add(src)

def _segment_sum(src, seg, n):
    return jax.ops.segment_sum(src, seg, n)
kernel_name = 'mk_xattn_seq_d4_seqx_r4_ec5162'

def setup_inputs(seed: int=0):
    np.random.seed(seed)
    _w = jnp.asarray

    def _rec_inputs():
        import jax
        import jax.numpy as jnp
        _rk = jax.random.key(seed)
        x = -0.0003929 + 0.9999 * jax.random.normal(jax.random.fold_in(_rk, 1), (8, 112, 256), jnp.float32)
        _lenS = 112 - jax.random.randint(jax.random.fold_in(_rk, 7), (8,), 0, max(1, 112 // 4) + 1, jnp.int32)
        _lenS2 = 375 - jax.random.randint(jax.random.fold_in(_rk, 8), (8,), 0, max(1, 375 // 4) + 1, jnp.int32)
        _ctx_512P = jax.random.normal(jax.random.fold_in(_rk, 11), (8, 16, 128), jnp.float32)
        _ctx_512c = jax.random.dirichlet(jax.random.fold_in(_rk, 511), 0.3 * jnp.ones((16,), jnp.float32), (8, 375))
        _ctx_512t = jnp.einsum('bsk,bkd->bsd', _ctx_512c, _ctx_512P)
        _ctx_512t = _ctx_512t * jax.lax.rsqrt(jnp.mean(jnp.square(_ctx_512t)) + 1e-12) * 0.953939
        ctx_512 = 4.13588e-05 + 0.999923 * (_ctx_512t + 0.3 * jax.random.normal(jax.random.fold_in(_rk, 611), (8, 375, 128), jnp.float32))
        _validS = jnp.arange(112)[None, :] < _lenS[:, None]
        _validS2 = jnp.arange(375)[None, :] < _lenS2[:, None]
        _causal = jnp.tril(jnp.ones((112, 112), dtype=bool))
        mask_BxSxS_ik0 = jnp.where(jnp.broadcast_to(_validS[:, None, :], (8, 112, 112)), 0, 1).astype(jnp.int32)
        mask_Bx1xS2_if1 = jnp.where(jnp.ones((8, 1, 375), dtype=bool), 1, 0).astype(jnp.int32)
        return (x, ctx_512, mask_BxSxS_ik0, mask_Bx1xS2_if1)
    x, ctx_512, mask_BxSxS_ik0, mask_Bx1xS2_if1 = _rec_inputs()

    def _L0_xattn_setup():
        import jax, jax.numpy as jnp
        import numpy as np
        QUERY_DIM = 256
        KEY_DIM = 128
        HIDDEN_DIM = 256
        B, LQ, LK = (8, 512, 512)
        key = jax.random.key(seed)
        ks = jax.random.split(key, 10)
        s_q = 1.0 / np.sqrt(QUERY_DIM)
        s_k = 1.0 / np.sqrt(KEY_DIM)
        s_h = 1.0 / np.sqrt(HIDDEN_DIM)
        return {'query': jax.random.normal(ks[0], (B, LQ, QUERY_DIM), jnp.float32), 'key': jax.random.normal(ks[1], (B, LK, KEY_DIM), jnp.float32), 'Wq': jax.random.uniform(ks[2], (QUERY_DIM, HIDDEN_DIM), jnp.float32, -s_q, s_q), 'bq': jax.random.uniform(ks[3], (HIDDEN_DIM,), jnp.float32, -s_q, s_q), 'Wk': jax.random.uniform(ks[4], (KEY_DIM, HIDDEN_DIM), jnp.float32, -s_k, s_k), 'bk': jax.random.uniform(ks[5], (HIDDEN_DIM,), jnp.float32, -s_k, s_k), 'Wv': jax.random.uniform(ks[6], (KEY_DIM, HIDDEN_DIM), jnp.float32, -s_k, s_k), 'bv': jax.random.uniform(ks[7], (HIDDEN_DIM,), jnp.float32, -s_k, s_k), 'Wo': jax.random.uniform(ks[8], (HIDDEN_DIM, QUERY_DIM), jnp.float32, -s_h, s_h), 'bo': jax.random.uniform(ks[9], (QUERY_DIM,), jnp.float32, -s_h, s_h)}
    _L0_xattn_all = _L0_xattn_setup()
    _L0_xattn_in = {k: v for k, v in _L0_xattn_all.items() if k in ('Wq', 'bq', 'Wk', 'bk', 'Wv', 'bv', 'Wo', 'bo')}
    del _L0_xattn_all

    def _L1_xattn_setup():
        import jax, jax.numpy as jnp
        import numpy as np
        B, T, E = (8, 1024, 256)
        M, L = (64, 128)
        EPS = 1e-06
        key = jax.random.key(seed)
        ks = jax.random.split(key, 5)
        return {'emb': jax.random.normal(ks[0], (B, T, E), dtype=jnp.float32), 'latent': jax.random.normal(ks[1], (B, M, L), dtype=jnp.float32), 'Wq': jax.random.normal(ks[2], (E, E), dtype=jnp.float32) * (1.0 / np.sqrt(E)), 'bq': jnp.zeros((E,), dtype=jnp.float32), 'Wk': jax.random.normal(ks[3], (L, E), dtype=jnp.float32) * (1.0 / np.sqrt(L)), 'bk': jnp.zeros((E,), dtype=jnp.float32), 'Wv': jax.random.normal(ks[4], (L, E), dtype=jnp.float32) * (1.0 / np.sqrt(L)), 'bv': jnp.zeros((E,), dtype=jnp.float32), 'gamma': jnp.ones((E,), dtype=jnp.float32), 'beta': jnp.zeros((E,), dtype=jnp.float32)}
    _L1_xattn_all = _L1_xattn_setup()
    _L1_xattn_in = {k: v for k, v in _L1_xattn_all.items() if k in ('Wq', 'bq', 'Wk', 'bk', 'Wv', 'bv', 'gamma', 'beta')}
    del _L1_xattn_all

    def _L2_xattn_setup():
        import jax, jax.numpy as jnp
        import numpy as np
        QUERY_DIM = 256
        KEY_DIM = 128
        HIDDEN_DIM = 256
        B, LQ, LK = (8, 512, 512)
        key = jax.random.key(seed)
        ks = jax.random.split(key, 10)
        s_q = 1.0 / np.sqrt(QUERY_DIM)
        s_k = 1.0 / np.sqrt(KEY_DIM)
        s_h = 1.0 / np.sqrt(HIDDEN_DIM)
        return {'query': jax.random.normal(ks[0], (B, LQ, QUERY_DIM), jnp.float32), 'key': jax.random.normal(ks[1], (B, LK, KEY_DIM), jnp.float32), 'Wq': jax.random.uniform(ks[2], (QUERY_DIM, HIDDEN_DIM), jnp.float32, -s_q, s_q), 'bq': jax.random.uniform(ks[3], (HIDDEN_DIM,), jnp.float32, -s_q, s_q), 'Wk': jax.random.uniform(ks[4], (KEY_DIM, HIDDEN_DIM), jnp.float32, -s_k, s_k), 'bk': jax.random.uniform(ks[5], (HIDDEN_DIM,), jnp.float32, -s_k, s_k), 'Wv': jax.random.uniform(ks[6], (KEY_DIM, HIDDEN_DIM), jnp.float32, -s_k, s_k), 'bv': jax.random.uniform(ks[7], (HIDDEN_DIM,), jnp.float32, -s_k, s_k), 'Wo': jax.random.uniform(ks[8], (HIDDEN_DIM, QUERY_DIM), jnp.float32, -s_h, s_h), 'bo': jax.random.uniform(ks[9], (QUERY_DIM,), jnp.float32, -s_h, s_h)}
    _L2_xattn_all = _L2_xattn_setup()
    _L2_xattn_in = {k: v for k, v in _L2_xattn_all.items() if k in ('Wq', 'bq', 'Wk', 'bk', 'Wv', 'bv', 'Wo', 'bo')}
    del _L2_xattn_all

    def _L3_xattn_setup():
        import jax, jax.numpy as jnp
        import numpy as np
        B, ST, SS = (8, 128, 144)
        TD, SD = (256, 128)
        L, H, D, FF = (6, 16, 64, 1024)

        def _ln(x, g, b, eps=1e-05):
            m = jnp.mean(x, axis=-1, keepdims=True)
            v = jnp.mean(jnp.square(x - m), axis=-1, keepdims=True)
            return (x - m) / jnp.sqrt(v + eps) * g + b

        def _heads(x):
            b, s, _ = x.shape
            return x.reshape(b, s, H, D).transpose(0, 2, 1, 3)

        def _mha(s, t, kv_w, q_w, o_w, o_b, mask):
            kv = s @ kv_w
            k, v = jnp.split(kv, 2, axis=-1)
            q = t @ q_w
            k, v, q = (_heads(k), _heads(v), _heads(q))
            scores = jnp.einsum('bhqd,bhkd->bhqk', q, k) * D ** (-0.5)
            scores = jnp.where(mask[:, None] == 0, jnp.float32(-1000000000.0), scores)
            attn = jax.nn.softmax(scores, axis=-1)
            o = jnp.einsum('bhqk,bhkd->bhqd', attn, v)
            o = o.transpose(0, 2, 1, 3).reshape(t.shape[0], t.shape[1], H * D)
            return o @ o_w + o_b
        key = jax.random.key(seed)
        ks = jax.random.split(key, 18)
        sc = 0.02
        inp = {'src': jax.random.normal(ks[0], (B, SS, SD), jnp.float32), 'tgt': jax.random.normal(ks[1], (B, ST, TD), jnp.float32), 'tgt_mask': jnp.broadcast_to(jnp.tril(jnp.ones((ST, ST), jnp.int32)), (B, ST, ST)), 'src_mask': jnp.ones((B, 1, SS), jnp.int32), 'norm_g': jnp.ones((TD,), jnp.float32), 'norm_b': jnp.zeros((TD,), jnp.float32), 'sa_kv': jax.random.normal(ks[2], (L, TD, 2 * H * D), jnp.float32) * sc, 'sa_q': jax.random.normal(ks[3], (L, TD, H * D), jnp.float32) * sc, 'sa_ow': jax.random.normal(ks[4], (L, H * D, TD), jnp.float32) * sc, 'sa_ob': jnp.zeros((L, TD), jnp.float32), 'ca_kv': jax.random.normal(ks[5], (L, SD, 2 * H * D), jnp.float32) * sc, 'ca_q': jax.random.normal(ks[6], (L, TD, H * D), jnp.float32) * sc, 'ca_ow': jax.random.normal(ks[7], (L, H * D, TD), jnp.float32) * sc, 'ca_ob': jnp.zeros((L, TD), jnp.float32), 'ff_w1': jax.random.normal(ks[8], (L, TD, FF), jnp.float32) * sc, 'ff_b1': jnp.zeros((L, FF), jnp.float32), 'ff_w2': jax.random.normal(ks[9], (L, FF, TD), jnp.float32) * sc, 'ff_b2': jnp.zeros((L, TD), jnp.float32), 'pre_g': jnp.ones((L, TD), jnp.float32), 'pre_b': jnp.zeros((L, TD), jnp.float32)}
        return inp
    _L3_xattn_all = _L3_xattn_setup()
    _L3_xattn_in = {k: v for k, v in _L3_xattn_all.items() if k in ('norm_g', 'norm_b', 'sa_kv', 'sa_q', 'sa_ow', 'sa_ob', 'ca_kv', 'ca_q', 'ca_ow', 'ca_ob', 'ff_w1', 'ff_b1', 'ff_w2', 'ff_b2', 'pre_g', 'pre_b')}
    del _L3_xattn_all
    return {'x': x, 'ctx_512': ctx_512, 'mask_BxSxS_ik0': mask_BxSxS_ik0, 'mask_Bx1xS2_if1': mask_Bx1xS2_if1, 'L0_xattn_Wq': _L0_xattn_in['Wq'], 'L0_xattn_bq': _L0_xattn_in['bq'], 'L0_xattn_Wk': _L0_xattn_in['Wk'], 'L0_xattn_bk': _L0_xattn_in['bk'], 'L0_xattn_Wv': _L0_xattn_in['Wv'], 'L0_xattn_bv': _L0_xattn_in['bv'], 'L0_xattn_Wo': _L0_xattn_in['Wo'], 'L0_xattn_bo': _L0_xattn_in['bo'], 'L1_xattn_Wq': _L1_xattn_in['Wq'], 'L1_xattn_bq': _L1_xattn_in['bq'], 'L1_xattn_Wk': _L1_xattn_in['Wk'], 'L1_xattn_bk': _L1_xattn_in['bk'], 'L1_xattn_Wv': _L1_xattn_in['Wv'], 'L1_xattn_bv': _L1_xattn_in['bv'], 'L1_xattn_gamma': _L1_xattn_in['gamma'], 'L1_xattn_beta': _L1_xattn_in['beta'], 'L2_xattn_Wq': _L2_xattn_in['Wq'], 'L2_xattn_bq': _L2_xattn_in['bq'], 'L2_xattn_Wk': _L2_xattn_in['Wk'], 'L2_xattn_bk': _L2_xattn_in['bk'], 'L2_xattn_Wv': _L2_xattn_in['Wv'], 'L2_xattn_bv': _L2_xattn_in['bv'], 'L2_xattn_Wo': _L2_xattn_in['Wo'], 'L2_xattn_bo': _L2_xattn_in['bo'], 'L3_xattn_norm_g': _L3_xattn_in['norm_g'], 'L3_xattn_norm_b': _L3_xattn_in['norm_b'], 'L3_xattn_sa_kv': _L3_xattn_in['sa_kv'], 'L3_xattn_sa_q': _L3_xattn_in['sa_q'], 'L3_xattn_sa_ow': _L3_xattn_in['sa_ow'], 'L3_xattn_sa_ob': _L3_xattn_in['sa_ob'], 'L3_xattn_ca_kv': _L3_xattn_in['ca_kv'], 'L3_xattn_ca_q': _L3_xattn_in['ca_q'], 'L3_xattn_ca_ow': _L3_xattn_in['ca_ow'], 'L3_xattn_ca_ob': _L3_xattn_in['ca_ob'], 'L3_xattn_ff_w1': _L3_xattn_in['ff_w1'], 'L3_xattn_ff_b1': _L3_xattn_in['ff_b1'], 'L3_xattn_ff_w2': _L3_xattn_in['ff_w2'], 'L3_xattn_ff_b2': _L3_xattn_in['ff_b2'], 'L3_xattn_pre_g': _L3_xattn_in['pre_g'], 'L3_xattn_pre_b': _L3_xattn_in['pre_b']}

def reference(x, ctx_512, mask_BxSxS_ik0, mask_Bx1xS2_if1, L0_xattn_Wq, L0_xattn_bq, L0_xattn_Wk, L0_xattn_bk, L0_xattn_Wv, L0_xattn_bv, L0_xattn_Wo, L0_xattn_bo, L1_xattn_Wq, L1_xattn_bq, L1_xattn_Wk, L1_xattn_bk, L1_xattn_Wv, L1_xattn_bv, L1_xattn_gamma, L1_xattn_beta, L2_xattn_Wq, L2_xattn_bq, L2_xattn_Wk, L2_xattn_bk, L2_xattn_Wv, L2_xattn_bv, L2_xattn_Wo, L2_xattn_bo, L3_xattn_norm_g, L3_xattn_norm_b, L3_xattn_sa_kv, L3_xattn_sa_q, L3_xattn_sa_ow, L3_xattn_sa_ob, L3_xattn_ca_kv, L3_xattn_ca_q, L3_xattn_ca_ow, L3_xattn_ca_ob, L3_xattn_ff_w1, L3_xattn_ff_b1, L3_xattn_ff_w2, L3_xattn_ff_b2, L3_xattn_pre_g, L3_xattn_pre_b):
    import jax
    import jax.numpy as jnp

    def _L0_xattn_ref(query, key, Wq, bq, Wk, bk, Wv, bv, Wo, bo):
        import jax, jax.numpy as jnp
        import numpy as np
        QUERY_DIM = 256
        KEY_DIM = 128
        HIDDEN_DIM = 256
        B, LQ, LK = (8, 512, 512)
        scale = HIDDEN_DIM ** (-0.5)
        Q = jnp.einsum('bqd,dh->bqh', query, Wq) + bq
        K = jnp.einsum('bkd,dh->bkh', key, Wk) + bk
        V = jnp.einsum('bkd,dh->bkh', key, Wv) + bv
        scores = jnp.einsum('bqh,bkh->bqk', Q, K) * scale
        weights = jax.nn.softmax(scores, axis=-1)
        attended = jnp.einsum('bqk,bkh->bqh', weights, V)
        out = jnp.einsum('bqh,hd->bqd', attended, Wo) + bo
        return query + out

    def _L1_xattn_ref(emb, latent, Wq, bq, Wk, bk, Wv, bv, gamma, beta):
        import jax, jax.numpy as jnp
        import numpy as np
        B, T, E = (8, 1024, 256)
        M, L = (64, 128)
        EPS = 1e-06
        q = jnp.einsum('bte,ef->btf', emb, Wq) + bq
        k = jnp.einsum('bml,le->bme', latent, Wk) + bk
        v = jnp.einsum('bml,le->bme', latent, Wv) + bv
        scale = 1.0 / jnp.sqrt(jnp.asarray(E, dtype=q.dtype))
        w = jnp.einsum('bte,bme->btm', q, k) * scale
        w = jax.nn.softmax(w, axis=1)
        pred = jnp.einsum('btm,bme->bte', w, v)
        x = pred + emb
        mu = jnp.mean(x, axis=-1, keepdims=True)
        var = jnp.var(x, axis=-1, keepdims=True)
        return (x - mu) * jax.lax.rsqrt(var + EPS) * gamma + beta

    def _L2_xattn_ref(query, key, Wq, bq, Wk, bk, Wv, bv, Wo, bo):
        import jax, jax.numpy as jnp
        import numpy as np
        QUERY_DIM = 256
        KEY_DIM = 128
        HIDDEN_DIM = 256
        B, LQ, LK = (8, 512, 512)
        scale = HIDDEN_DIM ** (-0.5)
        Q = jnp.einsum('bqd,dh->bqh', query, Wq) + bq
        K = jnp.einsum('bkd,dh->bkh', key, Wk) + bk
        V = jnp.einsum('bkd,dh->bkh', key, Wv) + bv
        scores = jnp.einsum('bqh,bkh->bqk', Q, K) * scale
        weights = jax.nn.softmax(scores, axis=-1)
        attended = jnp.einsum('bqk,bkh->bqh', weights, V)
        out = jnp.einsum('bqh,hd->bqd', attended, Wo) + bo
        return query + out

    def _L3_xattn_ref(src, tgt, tgt_mask, src_mask, norm_g, norm_b, sa_kv, sa_q, sa_ow, sa_ob, ca_kv, ca_q, ca_ow, ca_ob, ff_w1, ff_b1, ff_w2, ff_b2, pre_g, pre_b):
        import jax, jax.numpy as jnp
        import numpy as np
        B, ST, SS = (8, 128, 144)
        TD, SD = (256, 128)
        L, H, D, FF = (6, 16, 64, 1024)

        def _ln(x, g, b, eps=1e-05):
            m = jnp.mean(x, axis=-1, keepdims=True)
            v = jnp.mean(jnp.square(x - m), axis=-1, keepdims=True)
            return (x - m) / jnp.sqrt(v + eps) * g + b

        def _heads(x):
            b, s, _ = x.shape
            return x.reshape(b, s, H, D).transpose(0, 2, 1, 3)

        def _mha(s, t, kv_w, q_w, o_w, o_b, mask):
            kv = s @ kv_w
            k, v = jnp.split(kv, 2, axis=-1)
            q = t @ q_w
            k, v, q = (_heads(k), _heads(v), _heads(q))
            scores = jnp.einsum('bhqd,bhkd->bhqk', q, k) * D ** (-0.5)
            scores = jnp.where(mask[:, None] == 0, jnp.float32(-1000000000.0), scores)
            attn = jax.nn.softmax(scores, axis=-1)
            o = jnp.einsum('bhqk,bhkd->bhqd', attn, v)
            o = o.transpose(0, 2, 1, 3).reshape(t.shape[0], t.shape[1], H * D)
            return o @ o_w + o_b
        stacked = (sa_kv, sa_q, sa_ow, sa_ob, ca_kv, ca_q, ca_ow, ca_ob, ff_w1, ff_b1, ff_w2, ff_b2, pre_g, pre_b)

        def step(t, p):
            skv, sq, sow, sob, ckv, cq, cow, cob, w1, b1, w2, b2, pg, pb = p
            tn = _ln(t, norm_g, norm_b)
            t = _mha(tn, tn, skv, sq, sow, sob, tgt_mask) + t
            tn = _ln(t, norm_g, norm_b)
            t = _mha(src, tn, ckv, cq, cow, cob, src_mask) + t
            tn = _ln(t, pg, pb)
            t = t + (jax.nn.relu(tn @ w1 + b1) @ w2 + b2)
            return (t, None)
        out, _ = jax.lax.scan(step, tgt, stacked)
        return out
    x = _L0_xattn_ref(x, ctx_512, L0_xattn_Wq, L0_xattn_bq, L0_xattn_Wk, L0_xattn_bk, L0_xattn_Wv, L0_xattn_bv, L0_xattn_Wo, L0_xattn_bo)
    x = _L1_xattn_ref(x, ctx_512, L1_xattn_Wq, L1_xattn_bq, L1_xattn_Wk, L1_xattn_bk, L1_xattn_Wv, L1_xattn_bv, L1_xattn_gamma, L1_xattn_beta)
    x = _L2_xattn_ref(x, ctx_512, L2_xattn_Wq, L2_xattn_bq, L2_xattn_Wk, L2_xattn_bk, L2_xattn_Wv, L2_xattn_bv, L2_xattn_Wo, L2_xattn_bo)
    x = _L3_xattn_ref(ctx_512, x, mask_BxSxS_ik0, mask_Bx1xS2_if1, L3_xattn_norm_g, L3_xattn_norm_b, L3_xattn_sa_kv, L3_xattn_sa_q, L3_xattn_sa_ow, L3_xattn_sa_ob, L3_xattn_ca_kv, L3_xattn_ca_q, L3_xattn_ca_ow, L3_xattn_ca_ob, L3_xattn_ff_w1, L3_xattn_ff_b1, L3_xattn_ff_w2, L3_xattn_ff_b2, L3_xattn_pre_g, L3_xattn_pre_b)
    return x

_drawn_inputs = setup_inputs


def setup_inputs(seed=0):
    import zlib

    import numpy as np

    out = dict(_drawn_inputs(seed))
    spreads = {'L1_xattn_bq': (0.0, 0.8),
     'L1_xattn_bk': (0.0, 0.1),
     'L1_xattn_bv': (0.0, 0.1),
     'L1_xattn_gamma': (1.0, 0.2),
     'L1_xattn_beta': (0.0, 0.1),
     'L3_xattn_norm_g': (1.0, 0.2),
     'L3_xattn_norm_b': (0.0, 0.1),
     'L3_xattn_sa_ob': (0.0, 0.1),
     'L3_xattn_ca_ob': (0.0, 0.1),
     'L3_xattn_ff_b1': (0.0, 0.1),
     'L3_xattn_ff_b2': (0.0, 0.1),
     'L3_xattn_pre_g': (1.0, 0.2),
     'L3_xattn_pre_b': (0.0, 0.274)}
    factors = {'L0_xattn_Wq': 4.821,
     'L0_xattn_bq': 8.0,
     'L0_xattn_Wk': 4.83,
     'L0_xattn_bk': 8.0,
     'L0_xattn_bv': 3.901,
     'L0_xattn_bo': 2.985,
     'L2_xattn_Wq': 3.093,
     'L2_xattn_bq': 8.0,
     'L2_xattn_Wk': 3.117,
     'L2_xattn_bk': 8.0,
     'L3_xattn_sa_q': 8.0,
     'L3_xattn_ca_q': 8.0}
    for name, (base, spread) in spreads.items():
        noise = np.random.default_rng([zlib.crc32(name.encode()), seed]).standard_normal(out[name].shape)
        drawn = base * np.exp(spread * noise) if base else spread * noise
        out[name] = jnp.asarray(drawn.astype(out[name].dtype))
    for name, factor in factors.items():
        out[name] = (out[name] * factor).astype(out[name].dtype)
    return out
```

```python
import concourse.bass as bass
from concourse import mybir
from contextlib import ExitStack


def attention_layers(nc, x, ctx_nat, ctx_tr, self_mask, ctx_mask, front, dec, out):
    f32, i32 = mybir.dt.float32, mybir.dt.int32
    ALU, ACT, AX = mybir.AluOpType, mybir.ActivationFunctionType, mybir.AxisListType
    ds = bass.ds

    B, S, E = x.shape
    _, S2, C = ctx_nat.shape
    L, _, HDIM = dec["sa_q"].shape
    P = 128
    EK = E // P
    D = 64
    H = HDIM // D
    HC = HDIM // P
    FC = dec["ff_w1"].shape[2] // P
    NB = 2
    PAIRS = B // NB
    T2 = NB * S
    KJ = 3
    KR = S2 // KJ
    G = 4
    GB = H // G
    SG = NB * GB
    NH = NB * H
    V2 = HDIM // 512
    FRONT_SCALE = float(E) ** -0.5
    SCALE = float(D) ** -0.5
    MASKED = -1.0e9 / SCALE

    FRONT = {"proj0": 14, "proj1": 14, "score0": 3, "score1": 3, "tr0": 2, "tr1": 2, "sum0": 3, "sum1": 3,
             "stats": 1, "tn": 1, "resid": 2, "negmax": 3 * NB, "exp": 3 * NB, "prob": 3 * NB,
             "dve": 4 * NB + 3, "pool": 1}
    SA_OUT = HC + V2
    CA_OUT = SA_OUT + 1 + 3 * HC // 2
    FF_OUT = CA_OUT + 1 + FC // 2
    MAIN = {"proj0": FF_OUT + 1, "proj1": FF_OUT + 1, "score0": (SG + NH) // 2, "score1": (SG + NH) // 2,
            "tr0": (SG + NH) // 2, "tr1": (SG + NH) // 2, "sum0": SG, "sum1": SG,
            "stats": 3, "tn": 3 * NB, "resid": 3, "negmax": SG + NH, "exp": SG + NH,
            "prob": SG + NH, "dve": 3 + 1 + 2 * SG + NH, "pool": 3}

    class Place:

        def __init__(self, main, it):
            self.main, self.it, self.n = main, it, {}

        def base(self, name):
            if self.main:
                return PAIRS * FRONT.get(name, 0) + self.it * MAIN[name]
            return self.it * FRONT[name]

        def at(self, name, k):
            return self.base(name) + k

        def emptied(self, name, k):
            return self.base(name) + k + 1

        def next(self, name):
            self.n[name] = self.n.get(name, 0) + 1
            return self.n[name] - 1

        def check(self):
            want = MAIN if self.main else FRONT
            for name, n in self.n.items():
                assert n == want[name], (name, n, want[name])

    scope = ExitStack()
    with scope:
        def sb(name, shape, dt=f32):
            return scope.enter_context(nc.sbuf_tensor(name, shape, dt))

        def sem(name):
            return scope.enter_context(nc.semaphore(name))

        ident = sb("ident", [P, P])
        eps = sb("eps", [S, 2, NB])
        minus_half = sb("minus_half", [S, NB])
        masked = sb("masked", [S, 1])
        t_all = sb("t_all", [S, B, E])
        ctxT = sb("ctxT", [P, B * S2])
        ctxN = sb("ctxN", [KR, NB, KJ, C])
        w_q = sb("w_q", [P, EK, HDIM])
        w_kv = sb("w_kv", [P, EK, 2 * HDIM])
        w_o = sb("w_o", [P, HC, E])
        c_q = sb("c_q", [P, EK, HDIM])
        c_kT = sb("c_kT", [P, HC, C])
        c_v = sb("c_v", [P, H, 2, D])
        c_o = sb("c_o", [P, HC, E])
        f_1 = sb("f_1", [P, EK, FC * P])
        f_2 = sb("f_2", [P, FC, E])
        f_b1 = sb("f_b1", [P, FC])
        norm = sb("norm", [P, 2, EK])
        pre = sb("pre", [P, 2, EK])
        o_bias = sb("o_bias", [S, 3, E])
        tw = sb("tw", [S, NB, E])
        tn = sb("tn", [S, NB, E])
        stats = sb("stats", [S, NB, 6])
        mv = sb("mv", [S, NB, 2])
        veps = sb("veps", [S, NB])
        rstd = sb("rstd", [S, NB])
        tnT = sb("tnT", [P, EK, T2])
        diag = sb("diag", [P, HC, 2, T2])
        qcT = sb("qcT", [P, H, T2])
        raw = sb("raw", [S, 2, S2])
        prob = sb("prob", [KR, 4, G * S])
        probT = sb("probT", [KR, 2, KJ, G * S])
        negmax = sb("negmax", [P, G * SG + NH])
        total = sb("total", [P, G * SG + NH])
        rtotal = sb("rtotal", [P, G * SG + NH])
        smask = sb("smask", [S, NB, S], i32)
        smask0 = sb("smask0", [S, NB, S], i32)
        cmask = sb("cmask", [P, NB, S2], i32)
        cbias = sb("cbias", [S, NB, S2])
        oT = sb("oT", [P, HC, T2])
        cT = sb("cT", [P, H, T2])
        q_flat = qcT[:, :, :].rearrange("p h t -> p (h t)")
        v_flat = cT[:, :, :].rearrange("p h t -> p (h t)")
        v = v_flat[0:S, 0:NB * HDIM].rearrange("p (b n) -> p b n", b=NB)
        qT = q_flat[:, 0:HC * T2].rearrange("p (c t) -> p c t", c=HC)
        hT = oT
        FW = 2 * EK * E + 2 * E
        fw = [q_flat[:, 0:FW], q_flat[:, FW:2 * FW], v_flat[:, 0:FW]]
        fwq = [a[:, 0:EK * E].rearrange("p (k n) -> p k n", k=EK) for a in fw]
        fwo = [a[:, EK * E:2 * EK * E].rearrange("p (k n) -> p k n", k=EK) for a in fw]
        fwk = [a[:, 2 * EK * E:2 * EK * E + E] for a in fw]
        fwv = [a[:, 2 * EK * E + E:FW] for a in fw]
        fkT = v_flat[:, FW:FW + NB * EK * S2].rearrange("p (b k n) -> p b k n", b=NB, k=EK)
        fqT = v_flat[:, FW + NB * EK * S2:FW + NB * EK * S2 + EK * T2].rearrange("p (k n) -> p k n", k=EK)
        fcT = oT[:, 0, :]
        faT = oT[:, 1:1 + EK, :]
        fcol = sb("fcol", [P, 3, 3, EK])
        fbias = sb("fbias", [P, 5, E])

        banks = {n: scope.enter_context(nc.psum_tensor(n, [P, 512], f32))
                 for n in ("proj0", "proj1", "score0", "score1", "tr0", "tr1", "sum0", "sum1")}
        ready = {n: sem(f"{n}_ready") for n in banks}
        taken = {n: sem(f"{n}_taken") for n in banks if "score" not in n}

        setup_ids = sem("setup_ids")
        setup_done = sem("setup_done")
        front_loaded = sem("front_loaded")
        x_loaded = sem("x_loaded")
        ctx_loaded = sem("ctx_loaded")
        mask_loaded = sem("mask_loaded")
        mask_used = sem("mask_used")
        front_done = sem("front_done")
        loaded = {n: sem(f"{n}_loaded") for n in
                  ("w_q", "w_kv", "w_o", "c_q", "c_kT", "c_v", "c_o", "f_1", "f_2", "small")}
        dve_step = sem("dve_step")
        pool_step = sem("pool_step")
        passed = sem("passed")
        stats_ready = sem("stats_ready")
        rstd_ready = sem("rstd_ready")
        tn_ready = sem("tn_ready")
        resid_ready = sem("resid_ready")
        negmax_ready = sem("negmax_ready")
        exp_ready = sem("exp_ready")
        rtotal_ready = sem("rtotal_ready")
        prob_ready = sem("prob_ready")
        stored = sem("stored")

        SMALL = 6
        FRONT_DMAS = 3 * 6 + 2 + 1 + 5 + 2

        block = scope.enter_context(nc.Block())

        @block.sync
        def _(sp):
            def spread(a, rows):
                return a.partition_broadcast(rows)

            def load_pair_x(p):
                sp.dma_start(tw[:, :, :], x[ds(p * NB, NB)].rearrange("b s e -> s b e")).then_inc(x_loaded, 16)
                sp.dma_start(cmask[:, :, :], ctx_mask[ds(p * NB, NB)].partition_broadcast(P)).then_inc(x_loaded, 16)

            def load_pair_ctx(p):
                sp.dma_start(ctxN[:, :, :, :], ctx_nat[ds(p * NB, NB)].rearrange("b (j r) c -> r b j c", r=KR))\
                    .then_inc(ctx_loaded, 16)

            def load_pair_masks(p):
                sp.dma_start(smask[:, :, :], self_mask[ds(p * NB, NB)].rearrange("b q k -> q b k")).then_inc(mask_loaded, 16)
                sp.dma_start(cmask[:, :, :], ctx_mask[ds(p * NB, NB)].partition_broadcast(P)).then_inc(mask_loaded, 16)

            def chunks(a, l):
                return a[ds(l, 1)].rearrange("o (k p) n -> p (o k) n", p=P)

            def load_sa(l):
                sp.dma_start(w_q[:, :, :], chunks(dec["sa_q"], l)).then_inc(loaded["w_q"], 16)
                sp.dma_start(w_kv[:, :, :], chunks(dec["sa_kv"], l)).then_inc(loaded["w_kv"], 16)
                sp.dma_start(w_o[:, :, :], chunks(dec["sa_ow"], l)).then_inc(loaded["w_o"], 16)

            def load_ca(l):
                sp.dma_start(c_q[:, :, :], chunks(dec["ca_q"], l)).then_inc(loaded["c_q"], 16)
                sp.dma_start(c_kT[:, :, :], chunks(dec["ca_kT"], l)).then_inc(loaded["c_kT"], 16)
                values = dec["ca_kv"][ds(l, 1), :, HDIM:2 * HDIM].rearrange("o c (h t d) -> c (o h) t d", t=2, d=D)
                for half in range(2):
                    sp.dma_start(c_v[:, half::2, half, :], values[:, :, half, :]).then_inc(loaded["c_v"], 16)
                sp.dma_start(c_o[:, :, :], chunks(dec["ca_ow"], l)).then_inc(loaded["c_o"], 16)

            def load_ff(l):
                sp.dma_start(f_1[:, :, :], chunks(dec["ff_w1"], l)).then_inc(loaded["f_1"], 16)
                sp.dma_start(f_2[:, :, :], chunks(dec["ff_w2"], l)).then_inc(loaded["f_2"], 16)

            def load_small(l):
                sp.dma_start(f_b1[:, :], dec["ff_b1"][ds(l, 1)].rearrange("o p k -> p (o k)")).then_inc(loaded["small"], 16)
                for n, name in enumerate(("pre_g", "pre_b")):
                    sp.dma_start(pre[:, n, :], dec[name][ds(l, 1)].rearrange("o p k -> p (o k)"))\
                        .then_inc(loaded["small"], 16)
                for n, name in enumerate(("sa_ob", "ca_ob", "ff_b2")):
                    sp.dma_start(o_bias[:, n, :], dec[name][ds(l, 1)].partition_broadcast(S)).then_inc(loaded["small"], 16)

            load_pair_x(0)
            for n in range(3):
                sp.dma_start(fwq[n], front[n]["Wq"].rearrange("(k p) n -> p k n", p=P)).then_inc(front_loaded, 16)
                sp.dma_start(fwk[n], front[n]["Wk"]).then_inc(front_loaded, 16)
                for j, name in enumerate(("bq", "bk", "bv")):
                    sp.dma_start(fcol[:, n, j, :], front[n][name]).then_inc(front_loaded, 16)
                if n == 0:
                    sp.dma_start(ctxT[:, :], ctx_tr).then_inc(front_loaded, 16)
                    load_pair_ctx(0)
                sp.dma_start(fwv[n], front[n]["Wv"]).then_inc(front_loaded, 16)
                if n != 1:
                    sp.dma_start(fwo[n], front[n]["Wo"].rearrange("(k p) n -> p k n", p=P)).then_inc(front_loaded, 16)
            for n, a in enumerate((front[0]["bo"], front[2]["bo"], front[1]["bv_row"], front[1]["gamma"], front[1]["beta"])):
                sp.dma_start(fbias[:, n, :], spread(a, P)).then_inc(front_loaded, 16)
            for n, name in enumerate(("norm_g", "norm_b")):
                sp.dma_start(norm[:, n, :], dec[name]).then_inc(front_loaded, 16)
            load_sa(0)
            sp.wait_ge(setup_done, 1)
            load_ca(0)
            load_ff(0)
            load_small(0)
            with sp.Fori(1, PAIRS) as p:
                sp.wait_ge(front_done, p)
                load_pair_x(p)
                load_pair_ctx(p)
            sp.wait_ge(front_done, PAIRS)
            load_pair_ctx(0)
            load_pair_masks(0)

            def next_pair(at, p):
                sp.wait_ge(mask_used, at.it * 2 + 2)
                load_pair_masks(p)
                sp.wait_ge(ready["proj1"], at.at("proj1", CA_OUT + 1))
                load_pair_ctx(p)

            def layer(l, last):
                with sp.Fori(1, PAIRS) as p:
                    next_pair(Place(True, l * PAIRS + p - 1), p)
                if last:
                    return
                at = Place(True, l * PAIRS + PAIRS - 1)
                sp.wait_ge(ready["proj1"], at.at("proj1", SA_OUT + 1))
                load_sa(l + 1)
                next_pair(at, 0)
                load_ca(l + 1)
                sp.wait_ge(taken["proj1"], at.emptied("proj1", FF_OUT + 1))
                load_small(l + 1)
                load_ff(l + 1)

            with sp.Fori(0, L - 1) as l:
                layer(l, False)
            layer(L - 1, True)
            sp.wait_ge(taken["proj1"], Place(True, L * PAIRS).emptied("proj1", 0))
            sp.dma_start(out.rearrange("b s e -> s b e"), t_all[:, :, :]).then_inc(stored, 16)
            sp.wait_ge(stored, 16)

        @block.gpsimd
        def _(pool):
            pool.memset(ident[:, :], 0.0).then_inc(setup_ids, 1)
            pool.memset(eps[:, 0, :], 1e-5)
            pool.memset(eps[:, 1, :], 1e-6)
            pool.memset(minus_half[:, :], -0.5)
            pool.memset(masked[:, :], MASKED)
            pool.memset(cbias[:, :, :], 0.0)
            pool.memset(c_v[:, :, :, :], 0.0)
            pool.memset(diag[:, :, :, :], 0.0).then_inc(setup_ids, 1)
            pool.wait_ge(setup_ids, 2)
            pool.affine_select(out=ident[:, :], in_=ident[:, :], compare_op=ALU.not_equal, fill=1.0, base=0,
                               pattern=[[-1, P]], channel_multiplier=1).then_inc(setup_done, 1)
            for name in taken:
                pool.sem_inc(taken[name], 1)

            def inverse_std(at, which):
                k = at.next("stats")
                pool.wait_ge(stats_ready, at.at("stats", k + 1))
                pool.tensor_tensor(veps[:, :], mv[:, :, 1], eps[:, which, :], ALU.add).then_inc(pool_step, 1)
                pool.wait_ge(pool_step, at.at("pool", at.next("pool") + 1))
                pool.tensor_tensor(rstd[:, :], veps[:, :], minus_half[:, :], ALU.pow).then_inc(rstd_ready, 1)

            def add_bias(bias):
                pool.tensor_tensor(tw[:, :, :], tw[:, :, :], bias.unsqueeze(1).broadcast_to([S, NB, E]), ALU.add)\
                    .then_inc(resid_ready, 1)

            pool.wait_ge(front_loaded, 16 * FRONT_DMAS)
            with pool.Fori(0, PAIRS) as p:
                at = Place(False, p)
                pool.wait_ge(ready["proj0"], at.at("proj0", 1))
                add_bias(fbias[0:S, 0, :])
                inverse_std(at, 1)
                pool.wait_ge(ready["proj0"], at.at("proj0", 10))
                add_bias(fbias[0:S, 1, :])

            with pool.Fori(0, L) as l:
                with pool.Fori(0, PAIRS) as p:
                    at = Place(True, l * PAIRS + p)
                    for n in range(3):
                        inverse_std(at, 0)
                        if n == 0:
                            pool.wait_ge(loaded["small"], (l + 1) * (16 * SMALL))
                        pool.wait_ge(tn_ready, at.at("tn", NB * (n + 1)))
                        add_bias(o_bias[:, n, :])
                        if n == 0:
                            for g in range(SG):
                                pr = prob[0:S, g % 4, :].rearrange("p (h k) -> p h k", h=G)
                                pool.wait_ge(rtotal_ready, (l * PAIRS + p) * SG + g + 1)
                                pool.tensor_tensor(pr, pr, rtotal[0:S, G * g:G * g + G].unsqueeze(2)
                                                   .broadcast_to([S, G, S]), ALU.mult).then_inc(prob_ready, 1)
                    at.check()

        @block.tensor
        def _(pe):
            def fill(at, name):
                if name in taken:
                    pe.wait_ge(taken[name], at.emptied(name, at.next(name)))
                return banks[name]

            def done(ins, name):
                ins.then_inc(ready[name], 1)

            def transposes_of(at, a):
                bank = fill(at, "proj0")
                for k in range(EK):
                    for b in range(NB):
                        ins = pe.transpose(bank[:, k * T2 + b * S:k * T2 + (b + 1) * S], a[:, b, k * P:(k + 1) * P],
                                           ident[0:S, 0:S])
                done(ins, "proj0")

            def project(at, name, weights, moving):
                bank = fill(at, name)
                for k, (w, m) in enumerate(zip(weights, moving)):
                    ins = pe.matmul(bank[0:w.shape[1], 0:m.shape[1]], w, m, start=k == 0, stop=k == len(weights) - 1)
                done(ins, name)

            def out_rows(at, stationary, weights):
                bank = fill(at, "proj1")
                for b in range(NB):
                    terms = [(a[:, b * S:(b + 1) * S], w) for a, w in zip(stationary, weights)]
                    for k, (a, w) in enumerate(terms):
                        ins = pe.matmul(bank[0:S, b * E:(b + 1) * E], a, w, start=k == 0, stop=k == len(terms) - 1)
                done(ins, "proj1")

            pe.wait_ge(setup_done, 1)
            pe.wait_ge(front_loaded, 16 * FRONT_DMAS)
            with pe.Fori(0, PAIRS) as p:
                at = Place(False, p)
                pe.wait_ge(x_loaded, (p + 1) * 32)
                pe.wait_ge(ctx_loaded, (p + 1) * 16)
                for n in range(3):
                    if n == 1:
                        pe.wait_ge(taken["proj1"], at.emptied("proj1", at.n["proj1"]))
                    if n == 2:
                        pe.wait_ge(tn_ready, p + 1)
                    transposes_of(at, tw)
                    pe.wait_ge(taken["proj0"], at.emptied("proj0", at.n["proj0"]))
                    for e in range(EK):
                        project(at, f"proj{e}", [fwq[n][:, k, e * P:(e + 1) * P] for k in range(EK)],
                                [tnT[:, k, :] for k in range(EK)])
                    for b in range(NB):
                        for e in range(EK):
                            project(at, f"proj{e}", [fwk[n][:, e * P:(e + 1) * P]], [ctxT[:, ds(p * (NB * S2) + b * S2, S2)]])
                    for b in range(NB):
                        for e in range(EK):
                            pe.wait_ge(taken[f"proj{e}"], at.emptied(f"proj{e}", at.n[f"proj{e}"] - (NB - 1 - b)))
                        name = f"score{b}"
                        if n == 1:
                            pe.wait_ge(negmax_ready, at.at("negmax", b + 1))
                        elif n == 2:
                            pe.wait_ge(exp_ready, at.at("exp", NB + b + 1))
                        if n != 1:
                            project(at, name, [fqT[:, e, b * S:(b + 1) * S] for e in range(EK)],
                                    [fkT[:, b, e, :] for e in range(EK)])
                        else:
                            bank = banks[name]
                            for j in range(KJ):
                                for e in range(EK):
                                    ins = pe.matmul(bank[0:KR, j * S:(j + 1) * S], fkT[:, b, e, j * KR:(j + 1) * KR],
                                                    fqT[:, e, b * S:(b + 1) * S], start=e == 0, stop=e == EK - 1)
                            done(ins, name)
                    if n != 1:
                        for b in range(NB):
                            name = f"tr{b}"
                            pe.wait_ge(prob_ready, at.at("prob", NB * n + b + 1))
                            bank = fill(at, name)
                            for j in range(KJ):
                                ins = pe.transpose(bank[0:KR, j * S:(j + 1) * S], prob[0:S, b, j * KR:(j + 1) * KR],
                                                   ident[0:S, 0:S])
                            done(ins, name)
                    for b in range(NB):
                        if n != 1:
                            pe.wait_ge(taken[f"tr{b}"], at.emptied(f"tr{b}", at.n[f"tr{b}"]))
                        else:
                            pe.wait_ge(prob_ready, at.at("prob", NB * n + b + 1))
                        project(at, f"sum{b}", [ctxN[:, b, j, :] for j in range(KJ)],
                                [probT[:, b, j, 0:S] for j in range(KJ)])
                    for b in range(NB):
                        pe.wait_ge(taken[f"sum{b}"], at.emptied(f"sum{b}", at.n[f"sum{b}"]))
                    if n != 1:
                        for e in range(EK):
                            project(at, f"proj{e}", [fwv[n][:, e * P:(e + 1) * P]], [fcT])
                        for e in range(EK):
                            pe.wait_ge(taken[f"proj{e}"], at.emptied(f"proj{e}", at.n[f"proj{e}"]))
                        out_rows(at, [faT[:, e, :] for e in range(EK)], [fwo[n][:, e, :] for e in range(EK)])
                    else:
                        bank = fill(at, "proj1")
                        for b in range(NB):
                            o = bank[0:S, b * E:(b + 1) * E]
                            pe.matmul(o, fcT[:, b * S:(b + 1) * S], fwv[n], start=True, stop=False)
                            for j in range(KJ):
                                ins = pe.matmul(o, probT[:, b, j, 0:S], fbias[0:KR, 2, :], start=False, stop=j == KJ - 1)
                        done(ins, "proj1")
                at.check()
            pe.wait_ge(front_done, PAIRS)

            with pe.Fori(0, L) as l:
                with pe.Fori(0, PAIRS) as p:
                    it = l * PAIRS + p
                    at = Place(True, it)

                    def weights(name):
                        pe.wait_ge(loaded[name], (l + 1) * (32 if name == "c_v" else 16))

                    def normed(n):
                        pe.wait_ge(tn_ready, at.at("tn", NB * (n + 1)))
                        transposes_of(at, tn)
                        pe.wait_ge(taken["proj0"], at.emptied("proj0", at.n["proj0"]))

                    def chunked(w, m, chunks):
                        for c in range(chunks):
                            project(at, f"proj{c % 2}", [w[:, k, c * P:(c + 1) * P] for k in range(EK)],
                                    [m[:, k, :] for k in range(EK)])

                    def all_taken(*names):
                        for name in names:
                            pe.wait_ge(taken[name], at.emptied(name, at.n[name]))

                    normed(0)
                    weights("w_q")
                    chunked(w_q, tnT, HC)
                    weights("w_kv")
                    chunked(w_kv, tnT, HC)
                    for b in range(NB):
                        for n in range(V2):
                            at_cols = HDIM + n * 512
                            project(at, f"proj{n % 2}", [tnT[:, k, b * S:(b + 1) * S] for k in range(EK)],
                                    [w_kv[:, k, at_cols:at_cols + 512] for k in range(EK)])
                    all_taken("proj0", "proj1")
                    for t in range(SG + 3):
                        if t < SG:
                            b, c = t // GB, t % GB * 2
                            if t < 2:
                                pe.wait_ge(negmax_ready, at.base("negmax"))
                            else:
                                pe.wait_ge(exp_ready, at.at("exp", t - 1))
                            bank = banks[f"score{t % 2}"]
                            for n in range(2):
                                ins = pe.matmul(bank[0:S, n * T2:(n + 1) * T2], qT[:, c + n, b * S:(b + 1) * S],
                                                diag[:, c + n, :, b * S:(b + 1) * S], start=True, stop=True)
                            done(ins, f"score{t % 2}")
                        if 0 <= t - 2 < SG:
                            g = t - 2
                            pe.wait_ge(prob_ready, at.at("prob", g + 1))
                            bank = fill(at, f"tr{g % 2}")
                            for h in range(G):
                                ins = pe.transpose(bank[0:S, h * S:(h + 1) * S], prob[0:S, g % 4, h * S:(h + 1) * S],
                                                   ident[0:S, 0:S])
                            done(ins, f"tr{g % 2}")
                        if 0 <= t - 3 < SG:
                            g = t - 3
                            b, c = g // GB, g % GB * 2
                            pe.wait_ge(taken[f"tr{g % 2}"], at.emptied(f"tr{g % 2}", g // 2 + 1))
                            bank = fill(at, f"sum{g % 2}")
                            for n in range(2):
                                ins = pe.matmul(bank[:, n * T2:(n + 1) * T2], v[:, b, (c + n) * P:(c + n + 1) * P],
                                                probT[0:S, g % 2, 0, n * T2:(n + 1) * T2], start=True, stop=True)
                            done(ins, f"sum{g % 2}")
                    all_taken("sum0", "sum1")
                    weights("w_o")
                    out_rows(at, [oT[:, c, :] for c in range(HC)], [w_o[:, c, :] for c in range(HC)])

                    normed(1)
                    weights("c_q")
                    chunked(c_q, tnT, HC)
                    weights("c_kT")
                    for c in range(HC):
                        if c < 2:
                            all_taken("proj0", "proj1")
                        project(at, f"proj{c % 2}", [c_kT[:, c, :]], [diag[:, c, :, :].rearrange("p h t -> p (h t)")])
                    all_taken("proj0", "proj1")
                    pe.wait_ge(ctx_loaded, (it + PAIRS + 1) * 16)
                    for t in range(NH + 3):
                        if t < NH:
                            b, h = t // H, t % H
                            if t < 2:
                                pe.wait_ge(exp_ready, at.at("exp", SG))
                            else:
                                pe.wait_ge(negmax_ready, at.at("negmax", SG + t - 1))
                            project(at, f"score{t % 2}", [qcT[:, h, b * S:(b + 1) * S]],
                                    [ctxT[:, ds(p * (NB * S2) + b * S2, S2)]])
                        if 0 <= t - 2 < NH:
                            i = t - 2
                            pe.wait_ge(prob_ready, at.at("prob", SG + i + 1))
                            bank = fill(at, f"tr{i % 2}")
                            for j in range(KJ):
                                ins = pe.transpose(bank[0:KR, j * S:(j + 1) * S], prob[0:S, i % 4, j * KR:(j + 1) * KR],
                                                   ident[0:S, 0:S])
                            done(ins, f"tr{i % 2}")
                        if 0 <= t - 3 < NH and (t - 3) % G == G - 1:
                            g = (t - 3) // G
                            b = g // GB
                            for i in range(2):
                                pe.wait_ge(taken[f"tr{i}"], at.emptied(f"tr{i}", (SG + G * (g + 1)) // 2))
                            project(at, f"sum{g % 2}", [ctxN[:, b, j, :] for j in range(KJ)],
                                    [probT[:, g % 2, j, :] for j in range(KJ)])
                    all_taken("sum0", "sum1")
                    weights("c_v")
                    for c in range(HC):
                        project(at, f"proj{c % 2}", [c_v[:, 2 * c + n, :, :].rearrange("p t d -> p (t d)") for n in range(2)],
                                [cT[:, 2 * c + n, :] for n in range(2)])
                    all_taken("proj0", "proj1")
                    weights("c_o")
                    out_rows(at, [oT[:, c, :] for c in range(HC)], [c_o[:, c, :] for c in range(HC)])

                    normed(2)
                    weights("f_1")
                    chunked(f_1, tnT, FC)
                    all_taken("proj0", "proj1")
                    weights("f_2")
                    out_rows(at, [hT[:, c, :] for c in range(FC)], [f_2[:, c, :] for c in range(FC)])
                    at.check()

        @block.scalar
        def _(act):
            def filled(at, name):
                act.wait_ge(ready[name], at.at(name, at.next(name) + 1))
                return banks[name]

            def copy(o, i):
                return act.activation(o, i, ACT.Copy)

            def plus(o, i, bias):
                return act.activation(o, i, ACT.Identity, bias=bias)

            def softmax_row(at, k, o, i, scale, col):
                act.wait_ge(negmax_ready, at.at("negmax", k + 1))
                act.activation(o, i, ACT.Exp, bias=negmax[0:S, col:col + 1], scale=scale,
                               accum_out=total[0:S, col:col + 1]).then_inc(exp_ready, 1)

            act.wait_ge(setup_done, 1)
            act.wait_ge(front_loaded, 16 * FRONT_DMAS)
            with act.Fori(0, PAIRS) as p:
                at = Place(False, p)
                for n in range(3):
                    bank = filled(at, "proj0")
                    copy(tnT[:, :, :].rearrange("p k t -> p (k t)"), bank[:, 0:EK * T2]).then_inc(taken["proj0"], 1)
                    bank = filled(at, "proj0")
                    plus(fqT[:, 0, :], bank[:, 0:T2], fcol[:, n, 0, 0:1]).then_inc(taken["proj0"], 1)
                    for b in range(NB):
                        bank = filled(at, "proj0")
                        plus(fkT[:, b, 0, :], bank[:, 0:S2], fcol[:, n, 1, 0:1]).then_inc(taken["proj0"], 1)
                    for b in range(NB):
                        if n != 1:
                            softmax_row(at, NB * n + b, prob[0:S, b, 0:S2], raw[:, b, :], -1.0, b)
                        else:
                            bank = banks[f"score{b}"]
                            act.wait_ge(negmax_ready, at.at("negmax", NB * n + b + 1))
                            for j in range(KJ):
                                ins = act.activation(prob[0:KR, b, j * S:(j + 1) * S], bank[0:KR, j * S:(j + 1) * S],
                                                     ACT.Exp, bias=negmax[0:KR, NB + KJ * b + j:NB + KJ * b + j + 1],
                                                     scale=FRONT_SCALE,
                                                     accum_out=total[0:KR, NB + KJ * b + j:NB + KJ * b + j + 1])
                            ins.then_inc(exp_ready, 1)
                    if n != 1:
                        bank = filled(at, "tr0")
                        copy(probT[:, 0, :, 0:S], bank[0:KR, 0:KJ * S].rearrange("p (j s) -> p j s", j=KJ))\
                            .then_inc(taken["tr0"], 1)
                    bank = filled(at, "sum0")
                    copy(fcT[:, 0:S], bank[:, 0:S]).then_inc(taken["sum0"], 1)
                    if n != 1:
                        bank = filled(at, "proj0")
                        plus(faT[:, 0, :], bank[:, 0:T2], fcol[:, n, 2, 0:1]).then_inc(taken["proj0"], 1)

            with act.Fori(0, L) as l:
                with act.Fori(0, PAIRS) as p:
                    at = Place(True, l * PAIRS + p)

                    def normed(scale_bias):
                        bank = filled(at, "proj0")
                        for k in range(EK):
                            ins = act.activation(tnT[:, k, :], bank[:, k * T2:(k + 1) * T2], ACT.Identity,
                                                 scale=scale_bias[:, 0, k:k + 1], bias=scale_bias[:, 1, k:k + 1])
                        ins.then_inc(taken["proj0"], 1)

                    def chunk_diag(c):
                        bank = filled(at, "proj0")
                        for h in range(2):
                            ins = copy(diag[h * D:(h + 1) * D, c, h, :], bank[h * D:(h + 1) * D, 0:T2])
                        ins.then_inc(taken["proj0"], 1)

                    def chunk(o, i, func=ACT.Copy, **kw):
                        bank = filled(at, "proj0")
                        act.activation(o, bank[0:o.shape[0], 0:i], func, **kw).then_inc(taken["proj0"], 1)

                    normed(norm)
                    for c in range(0, HC, 2):
                        chunk(qT[:, c, :], T2)
                    for c in range(0, HC, 2):
                        chunk_diag(c)
                    for b in range(NB):
                        chunk(v[:, b, 0:512], 512)
                    for t in range(SG + 3):
                        if t < SG:
                            act.wait_ge(ready[f"tr{t % 2}"], at.at(f"tr{t % 2}", t // 2 - 1))
                            act.wait_ge(negmax_ready, at.at("negmax", t + 1))
                            bank = banks[f"score{t % 2}"]
                            for h in range(G):
                                col = G * t + h
                                ins = act.activation(prob[0:S, t % 4, h * S:(h + 1) * S], bank[0:S, h * S:(h + 1) * S],
                                                     ACT.Exp, bias=negmax[0:S, col:col + 1], scale=SCALE,
                                                     accum_out=total[0:S, col:col + 1])
                            ins.then_inc(exp_ready, 1)
                        if 0 <= t - 2 < SG and t % 2 == 0:
                            bank = filled(at, "tr0")
                            copy(probT[0:S, 0, 0, :], bank[0:S, 0:G * S]).then_inc(taken["tr0"], 1)
                        if 0 <= t - 3 < SG and (t - 3) % 2 == 0:
                            b, c = (t - 3) // GB, (t - 3) % GB * 2
                            bank = filled(at, "sum0")
                            for h in range(2):
                                r = slice(h * D, (h + 1) * D)
                                ins = copy(oT[r, c:c + 2, b * S:(b + 1) * S],
                                           bank[r, 0:2 * T2].rearrange("p (n h s) -> p n h s", n=2, h=2)[:, :, h, :])
                            ins.then_inc(taken["sum0"], 1)

                    normed(norm)
                    for c in range(0, HC, 2):
                        chunk_diag(c)
                    for c in range(0, HC, 2):
                        chunk(qcT[:, 2 * c:2 * c + 2, :].rearrange("p h t -> p (h t)"), 2 * T2)
                    for t in range(NH + 3):
                        if 0 <= t - 2 < NH and t % 2 == 0:
                            i = t - 2
                            if i % G == 0:
                                g = SG + i // G
                                act.wait_ge(ready[f"sum{g % 2}"], at.at(f"sum{g % 2}", g // 2))
                            bank = filled(at, "tr0")
                            copy(probT[:, i // G % 2, :, i % G * S:(i % G + 1) * S],
                                 bank[0:KR, 0:KJ * S].rearrange("p (j s) -> p j s", j=KJ)).then_inc(taken["tr0"], 1)
                        if t < NH:
                            k = SG + t
                            act.wait_ge(ready[f"tr{t % 2}"], at.at(f"tr{t % 2}", k // 2 - 1))
                            softmax_row(at, k, prob[0:S, t % 4, 0:S2], raw[:, t % 2, :], -1.0, G * SG + t)
                        if 0 <= t - 3 < NH and (t - 3) % (2 * G) == G - 1:
                            g = (t - 3) // G
                            b, h = g // GB, g % GB * G
                            bank = filled(at, "sum0")
                            copy(cT[:, h:h + G, b * S:(b + 1) * S], bank[:, 0:G * S].rearrange("p (h s) -> p h s", h=G))\
                                .then_inc(taken["sum0"], 1)
                    for c in range(0, HC, 2):
                        chunk(oT[:, c, :], T2)
                    act.wait_ge(loaded["small"], (l + 1) * (16 * SMALL))
                    normed(pre)
                    for c in range(0, FC, 2):
                        chunk(hT[:, c, :], T2, ACT.Relu, bias=f_b1[:, c:c + 1])
                    assert at.n["proj0"] == MAIN["proj0"] and at.n["tr0"] == MAIN["tr0"] and at.n["sum0"] == MAIN["sum0"]

        @block.vector
        def _(dve):
            def filled(at, name):
                dve.wait_ge(ready[name], at.at(name, at.next(name) + 1))
                return banks[name]

            def gate(s, value):
                dve.wait_ge(s, value)
                dve.sem_inc(passed, 1)

            def link(at, ins):
                ins.then_inc(dve_step, 1)
                gate(dve_step, at.at("dve", at.next("dve") + 1))

            def plus(o, i, bias):
                return dve.tensor_scalar(o, i, bias, None, ALU.add)

            def statistics(at):
                for b in range(NB):
                    ins = dve.bn_stats(stats[:, b, :], tw[:, b, :])
                link(at, ins)
                for b in range(NB):
                    ins = dve.bn_aggr(mv[:, b, :], stats[:, b, :])
                ins.then_inc(stats_ready, 1)
                dve.wait_ge(rstd_ready, at.at("stats", at.next("stats") + 1))

            def normalise(o, b):
                return dve.tensor_scalar(o, tw[:, b, :], mv[:, b, 0:1], rstd[:, b:b + 1], ALU.subtract, ALU.mult)

            dve.wait_ge(setup_done, 1)
            dve.wait_ge(front_loaded, 16 * FRONT_DMAS)
            with dve.Fori(0, PAIRS) as p:
                at = Place(False, p)
                dve.wait_ge(x_loaded, (p + 1) * 32)
                for n in range(3):
                    bank = filled(at, "proj1")
                    plus(fqT[:, 1, :], bank[:, 0:T2], fcol[:, n, 0, 1:2]).then_inc(taken["proj1"], 1)
                    for b in range(NB):
                        bank = filled(at, "proj1")
                        plus(fkT[:, b, 1, :], bank[:, 0:S2], fcol[:, n, 1, 1:2]).then_inc(taken["proj1"], 1)
                    for b in range(NB):
                        if n != 1:
                            k = at.next(f"score{b}")
                            gate(ready[f"score{b}"], at.at(f"score{b}", k + 1))
                            dve.tensor_tensor_reduce(out=raw[:, b, :], in0=banks[f"score{b}"][0:S, 0:S2], in1=cbias[:, b, :],
                                                     scale=-FRONT_SCALE, scalar=3.4e38, op0=ALU.add, op1=ALU.min,
                                                     accum_out=negmax[0:S, b:b + 1]).then_inc(negmax_ready, 1)
                        else:
                            bank = filled(at, f"score{b}")
                            cols = slice(NB + KJ * b, NB + KJ * (b + 1))
                            link(at, dve.reduce_max(rtotal[0:KR, cols],
                                                    bank[0:KR, 0:KJ * S].rearrange("p (j s) -> p j s", j=KJ), AX.X))
                            dve.tensor_scalar(negmax[0:KR, cols], rtotal[0:KR, cols], -FRONT_SCALE, None, ALU.mult)\
                                .then_inc(negmax_ready, 1)
                    for b in range(NB):
                        k = NB * n + b
                        if n != 1:
                            dve.wait_ge(exp_ready, at.at("exp", k + 1))
                            link(at, dve.reciprocal(rtotal[0:S, b:b + 1], total[0:S, b:b + 1]))
                            dve.tensor_scalar(prob[0:S, b, 0:S2], prob[0:S, b, 0:S2], rtotal[0:S, b:b + 1], None, ALU.mult)\
                                .then_inc(prob_ready, 1)
                        else:
                            cols = slice(NB + KJ * b, NB + KJ * (b + 1))
                            dve.wait_ge(exp_ready, at.at("exp", k + 1))
                            link(at, dve.reciprocal(rtotal[0:KR, cols], total[0:KR, cols]))
                            dve.tensor_tensor(probT[:, b, :, 0:S], prob[:, b, 0:KJ * S].rearrange("p (j s) -> p j s", j=KJ),
                                              rtotal[0:KR, cols].unsqueeze(2).broadcast_to([KR, KJ, S]), ALU.mult)\
                                .then_inc(prob_ready, 1)
                    if n != 1:
                        bank = filled(at, "tr1")
                        dve.tensor_copy(probT[:, 1, :, 0:S], bank[0:KR, 0:KJ * S].rearrange("p (j s) -> p j s", j=KJ))\
                            .then_inc(taken["tr1"], 1)
                    bank = filled(at, "sum1")
                    dve.tensor_copy(fcT[:, S:T2], bank[:, 0:S]).then_inc(taken["sum1"], 1)
                    if n != 1:
                        bank = filled(at, "proj1")
                        plus(faT[:, 1, :], bank[:, 0:T2], fcol[:, n, 2, 1:2]).then_inc(taken["proj1"], 1)
                        dve.wait_ge(resid_ready, at.at("resid", at.next("resid") + 1))
                    bank = filled(at, "proj1")
                    dve.tensor_tensor(tw[:, :, :], bank[0:S, 0:NB * E].rearrange("p (b e) -> p b e", b=NB), tw[:, :, :],
                                      ALU.add).then_inc(taken["proj1"], 1)
                    if n == 1:
                        dve.wait_ge(taken["proj1"], at.emptied("proj1", at.n["proj1"]))
                        statistics(at)
                        for b in range(NB):
                            ins = normalise(tn[:, b, :], b)
                        link(at, ins)
                        link(at, dve.tensor_tensor(tn[:, :, :], tn[:, :, :],
                                                   fbias[0:S, 3, :].unsqueeze(1).broadcast_to([S, NB, E]), ALU.mult))
                        dve.tensor_tensor(tw[:, :, :], tn[:, :, :],
                                          fbias[0:S, 4, :].unsqueeze(1).broadcast_to([S, NB, E]), ALU.add)\
                            .then_inc(tn_ready, 1)
                dve.wait_ge(taken["proj1"], at.emptied("proj1", at.n["proj1"]))
                dve.tensor_copy(t_all[:, ds(p * NB, NB), :], tw[:, :, :])
                pair_ctx = ctxT[:, ds(p * (NB * S2), NB * S2)]
                dve.scalar_tensor_tensor(pair_ctx, cmask[:, :, :].rearrange("p b s -> p (b s)"), 0.0, pair_ctx,
                                         ALU.not_equal, ALU.mult).then_inc(front_done, 1)

            dve.wait_ge(front_done, PAIRS)
            with dve.Fori(0, L) as l:
                with dve.Fori(0, PAIRS) as p:
                    it = l * PAIRS + p
                    at = Place(True, it)
                    tokens = ds(p * NB, NB)

                    def normed():
                        statistics(at)
                        for b in range(NB):
                            normalise(tn[:, b, :], b).then_inc(tn_ready, 1)

                    def chunk_diag(c):
                        bank = filled(at, "proj1")
                        for h in range(2):
                            ins = dve.tensor_copy(diag[h * D:(h + 1) * D, c, h, :], bank[h * D:(h + 1) * D, 0:T2])
                        ins.then_inc(taken["proj1"], 1)

                    def chunk(o, i):
                        bank = filled(at, "proj1")
                        dve.tensor_copy(o, bank[0:o.shape[0], 0:i]).then_inc(taken["proj1"], 1)

                    def residual(o):
                        dve.wait_ge(resid_ready, at.at("resid", at.next("resid") + 1))
                        bank = filled(at, "proj1")
                        dve.tensor_tensor(o, bank[0:S, 0:NB * E].rearrange("p (b e) -> p b e", b=NB), tw[:, :, :],
                                          ALU.add).then_inc(taken["proj1"], 1)

                    def after_residual():
                        dve.wait_ge(taken["proj1"], at.emptied("proj1", at.n.get("proj1", 0)))

                    after_residual()
                    link(at, dve.tensor_copy(tw[:, :, :], t_all[:, tokens, :]))
                    normed()
                    dve.wait_ge(mask_loaded, (it + 1) * 32)
                    dve.tensor_scalar(smask0[:, :, :], smask[:, :, :], 0.0, None, ALU.is_equal).then_inc(mask_used, 1)
                    dve.tensor_scalar(cbias[:, :, :], cmask[0:S, :, :], 0.0, MASKED, ALU.is_equal, ALU.mult)\
                        .then_inc(mask_used, 1)
                    for c in range(1, HC, 2):
                        chunk(qT[:, c, :], T2)
                    for c in range(1, HC, 2):
                        chunk_diag(c)
                    for b in range(NB):
                        chunk(v[:, b, 512:1024], 512)
                    gate(mask_used, it * 2 + 2)
                    for t in range(SG + 3):
                        if t < SG:
                            name = f"score{t % 2}"
                            b, cols = t // GB, slice(G * t, G * t + G)
                            k = at.next(name)
                            gate(ready[name], at.at(name, k + 1))
                            four = banks[name][0:S, 0:G * S].rearrange("p (h k) -> p h k", h=G)
                            link(at, dve.copy_predicated(four, smask0[:, b, :].unsqueeze(1).broadcast_to([S, G, S]),
                                                         masked[:, 0:1].unsqueeze(1).broadcast_to([S, G, S])))
                            link(at, dve.reduce_max(rtotal[0:S, cols], four, AX.X))
                            dve.tensor_scalar(negmax[0:S, cols], rtotal[0:S, cols], -SCALE, None, ALU.mult)\
                                .then_inc(negmax_ready, 1)
                        if 0 <= t - 1 < SG:
                            cols = slice(G * (t - 1), G * t)
                            dve.wait_ge(exp_ready, at.at("exp", t))
                            dve.reciprocal(rtotal[0:S, cols], total[0:S, cols]).then_inc(rtotal_ready, 1)
                        if 0 <= t - 2 < SG and t % 2 == 1:
                            bank = filled(at, "tr1")
                            dve.tensor_copy(probT[0:S, 1, 0, :], bank[0:S, 0:G * S]).then_inc(taken["tr1"], 1)
                        if 0 <= t - 3 < SG and (t - 3) % 2 == 1:
                            b, c = (t - 3) // GB, (t - 3) % GB * 2
                            bank = filled(at, "sum1")
                            for h in range(2):
                                r = slice(h * D, (h + 1) * D)
                                ins = dve.tensor_copy(oT[r, c:c + 2, b * S:(b + 1) * S],
                                                      bank[r, 0:2 * T2].rearrange("p (n h s) -> p n h s", n=2, h=2)[:, :, h, :])
                            ins.then_inc(taken["sum1"], 1)
                    residual(tw[:, :, :])

                    after_residual()
                    normed()
                    for c in range(1, HC, 2):
                        chunk_diag(c)
                    for c in range(1, HC, 2):
                        chunk(qcT[:, 2 * c:2 * c + 2, :].rearrange("p h t -> p (h t)"), 2 * T2)
                    for t in range(NH + 3):
                        if t < NH:
                            name = f"score{t % 2}"
                            col = G * SG + t
                            if t >= 2:
                                gate(exp_ready, at.at("exp", SG + t - 1))
                            gate(ready[name], at.at(name, at.next(name) + 1))
                            dve.tensor_tensor_reduce(out=raw[:, t % 2, :], in0=banks[name][0:S, 0:S2],
                                                     in1=cbias[:, t // H, :], scale=-SCALE, scalar=3.4e38,
                                                     op0=ALU.add, op1=ALU.min, accum_out=negmax[0:S, col:col + 1])\
                                .then_inc(negmax_ready, 1)
                        if 0 <= t - 1 < NH:
                            k = SG + t - 1
                            col = G * SG + t - 1
                            row = prob[0:S, (t - 1) % 4, 0:S2]
                            dve.wait_ge(exp_ready, at.at("exp", k + 1))
                            link(at, dve.reciprocal(rtotal[0:S, col:col + 1], total[0:S, col:col + 1]))
                            dve.tensor_scalar(row, row, rtotal[0:S, col:col + 1], None, ALU.mult).then_inc(prob_ready, 1)
                        if 0 <= t - 2 < NH and t % 2 == 1:
                            i = t - 2
                            if i % G == 1:
                                g = SG + i // G
                                dve.wait_ge(ready[f"sum{g % 2}"], at.at(f"sum{g % 2}", g // 2))
                            bank = filled(at, "tr1")
                            dve.tensor_copy(probT[:, i // G % 2, :, i % G * S:(i % G + 1) * S],
                                            bank[0:KR, 0:KJ * S].rearrange("p (j s) -> p j s", j=KJ)).then_inc(taken["tr1"], 1)
                        if 0 <= t - 3 < NH and (t - 3) % (2 * G) == 2 * G - 1:
                            g = (t - 3) // G
                            b, h = g // GB, g % GB * G
                            bank = filled(at, "sum1")
                            dve.tensor_copy(cT[:, h:h + G, b * S:(b + 1) * S],
                                            bank[:, 0:G * S].rearrange("p (h s) -> p h s", h=G)).then_inc(taken["sum1"], 1)
                    for c in range(1, HC, 2):
                        chunk(oT[:, c, :], T2)
                    residual(tw[:, :, :])

                    after_residual()
                    normed()
                    for c in range(1, FC, 2):
                        bank = filled(at, "proj1")
                        dve.tensor_scalar(hT[:, c, :], bank[:, 0:T2], f_b1[:, c:c + 1], 0.0, ALU.add, ALU.max)\
                            .then_inc(taken["proj1"], 1)
                    residual(t_all[:, tokens, :])
                    assert all(at.n[k] == MAIN[k] for k in ("proj1", "tr1", "sum1", "dve", "stats", "resid"))


_DECODER = ["sa_kv", "sa_q", "sa_ow", "sa_ob", "ca_kv", "ca_q", "ca_ow", "ca_ob", "ff_w1", "ff_b1", "ff_w2", "ff_b2",
            "pre_g", "pre_b", "norm_g", "norm_b"]
_COLUMNS = ("bq", "bk", "bv", "ff_b1", "pre_g", "pre_b", "norm_g", "norm_b")
_FRONT = [["Wq", "bq", "Wk", "bk", "Wv", "bv", "Wo", "bo"], ["Wq", "bq", "Wk", "bk", "Wv", "bv", "gamma", "beta"],
          ["Wq", "bq", "Wk", "bk", "Wv", "bv", "Wo", "bo"]]


def kernel(**inputs):
    import numpy as _np
    import concourse.bacc as _bacc
    from concourse import mybir as _mybir
    from concourse.bass_utils import run_bass_kernel_spmd as _run

    nc = _bacc.Bacc("TRN2", target_bir_lowering=False, num_devices=1)
    arrays = {}

    def give(name, a):
        a = _np.ascontiguousarray(a)
        arrays[name] = a
        return nc.dram_tensor(name, a.shape, _mybir.dt.from_np(a.dtype), kind="ExternalInput").ap()

    x = _np.asarray(inputs["x"])
    ctx = _np.asarray(inputs["ctx_512"])
    mask = _np.asarray(inputs["mask_Bx1xS2_if1"])
    hd = inputs["L3_xattn_sa_q"].shape[2]

    def columns(a):
        a = _np.asarray(a)
        return _np.swapaxes(a.reshape(a.shape[:-1] + (-1, 128)), -1, -2)

    dec = {n: give(n, (columns if n in _COLUMNS else _np.asarray)(inputs["L3_xattn_" + n])) for n in _DECODER}
    dec["ca_kT"] = give("ca_kT", _np.asarray(inputs["L3_xattn_ca_kv"])[:, :, 0:hd].transpose(0, 2, 1))
    front = [{n: give(f"L{i}_{n}", (columns if n in _COLUMNS else _np.asarray)(inputs[f"L{i}_xattn_{n}"])) for n in names}
             for i, names in enumerate(_FRONT)]
    front[1]["bv_row"] = give("L1_bv_row", _np.asarray(inputs["L1_xattn_bv"]))
    args = [give("x", x), give("ctx", ctx), give("ctx_T", ctx.reshape(-1, ctx.shape[2]).T),
            give("self_mask", _np.asarray(inputs["mask_BxSxS_ik0"])), give("ctx_mask", mask.reshape(mask.shape[0], -1))]
    out = nc.dram_tensor("out", x.shape, _mybir.dt.float32, kind="ExternalOutput").ap()
    attention_layers(nc, *args, front, dec, out)
    return _run(nc, [arrays], core_ids=[0]).results[0]["out"]
```

```python
import concourse.bass as bass
from concourse import mybir
from contextlib import ExitStack


def attention_layers(nc, x, ctx_nat, ctx_tr, self_mask, ctx_mask, front, dec, out):
    f32, i32 = mybir.dt.float32, mybir.dt.int32
    ALU, ACT, AX = mybir.AluOpType, mybir.ActivationFunctionType, mybir.AxisListType
    ds = bass.ds

    B, S, E = x.shape
    _, S2, C = ctx_nat.shape
    L, _, HDIM = dec["sa_q"].shape
    P = 128
    EK = E // P
    D = 64
    H = HDIM // D
    HC = HDIM // P
    FC = dec["ff_w1"].shape[2] // P
    NB = 2
    PAIRS = B // NB
    T2 = NB * S
    KJ = 3
    KR = S2 // KJ
    G = 4
    GB = H // G
    SG = NB * GB
    NH = NB * H
    V2 = HDIM // 512
    FRONT_SCALE = float(E) ** -0.5
    SCALE = float(D) ** -0.5
    MASKED = -1.0e9 / SCALE

    FRONT = {"proj0": 14, "proj1": 14, "score0": 3, "score1": 3, "tr0": 2, "tr1": 2, "sum0": 3, "sum1": 3,
             "stats": 1, "tn": 1, "resid": 2, "negmax": 3 * NB, "exp": 3 * NB, "prob": 3 * NB, "rtotal": 0,
             "dve": 4 * NB + 3, "pool": 1}
    SA_OUT = 0
    CA_OUT = 1 + V2 + 3 * HC // 2
    Q_END = CA_OUT + 1 + HC // 2
    FF_OUT = Q_END + FC // 2
    SA_LAG, CA_LAG = 3, 4
    SUM_LAG = 2
    PROBS, RAWS = 8, 3
    KEY_STEPS = {(1 if c < HC // 2 else NH - HC // 2) + c: c for c in range(HC)}
    EARLY = SA_LAG
    SUM_Q = SG + 2
    SUM_CA = SUM_Q + HC
    MAIN = {"proj0": FF_OUT - 1, "proj1": FF_OUT + 1, "score0": (SG + NH) // 2, "score1": (SG + NH) // 2,
            "tr0": (SG + NH) // 2, "tr1": (SG + NH) // 2, "sum0": SG + HC // 2 + 2, "sum1": SG + HC // 2 + 3,
            "stats": 3, "tn": 3 * NB, "resid": 3, "negmax": SG + NH, "exp": SG + NH,
            "prob": SG + NH, "rtotal": SG + NH, "dve": 3 + 2 * SG, "pool": 3}
    BETWEEN = {"proj0": 1 + V2 + HC, "proj1": V2 + HC, "stats": 1, "tn": NB, "dve": 1 + 2 * EARLY, "pool": 1}
    FRONT_LOOP, START, MAIN_LOOP = range(3)

    class Place:

        def __init__(self, part, it=0):
            self.part, self.it, self.n = part, it, {}

        def base(self, name):
            if self.part == FRONT_LOOP:
                return self.it * FRONT[name]
            if self.part == START:
                return PAIRS * FRONT[name]
            return PAIRS * FRONT[name] + BETWEEN.get(name, 0) + self.it * MAIN[name]

        def at(self, name, k):
            return self.base(name) + k

        def emptied(self, name, k):
            return self.base(name) + k + 1

        def next(self, name):
            self.n[name] = self.n.get(name, 0) + 1
            return self.n[name] - 1

        def check(self):
            want = (FRONT, BETWEEN, MAIN)[self.part]
            for name, n in self.n.items():
                assert n == want[name], (name, n, want[name])

    scope = ExitStack()
    with scope:
        def sb(name, shape, dt=f32):
            return scope.enter_context(nc.sbuf_tensor(name, shape, dt))

        def sem(name):
            return scope.enter_context(nc.semaphore(name))

        ident = sb("ident", [P, P])
        eps = sb("eps", [S, 2, NB])
        minus_half = sb("minus_half", [S, NB])
        masked = sb("masked", [S, 1])
        t_all = sb("t_all", [S, B, E])
        ctxT = sb("ctxT", [P, B * S2])
        ctxN = sb("ctxN", [KR, NB, KJ, C])
        w_q = sb("w_q", [P, EK, HDIM])
        w_kv = sb("w_kv", [P, EK, 2 * HDIM])
        w_o = sb("w_o", [P, HC, E])
        c_q = sb("c_q", [P, EK, HDIM])
        c_kT = sb("c_kT", [P, HC, C])
        c_v = sb("c_v", [P, H, 2, D])
        c_o = sb("c_o", [P, HC, E])
        f_1 = sb("f_1", [P, EK, FC * P])
        f_2 = sb("f_2", [P, FC, E])
        f_b1 = sb("f_b1", [P, FC])
        norm = sb("norm", [P, 2, EK])
        pre = sb("pre", [P, 2, EK])
        o_bias = sb("o_bias", [S, 3, E])
        tw = sb("tw", [S, NB, E])
        tn = sb("tn", [S, NB, E])
        stats = sb("stats", [S, NB, 6])
        mv = sb("mv", [S, NB, 2])
        veps = sb("veps", [S, NB])
        rstd = sb("rstd", [S, NB])
        tnT = sb("tnT", [P, EK, T2])
        tnT_next = sb("tnT_next", [P, EK, T2])
        k_diag = sb("k_diag", [P, HC, 2, T2])
        q_diag = k_diag
        v_all = sb("v", [P, NB * HDIM])
        v = v_all[0:S, :].rearrange("p (b n) -> p b n", b=NB)
        oT = sb("oT", [P, HC, T2])
        qT = oT
        qcT = sb("qcT", [P, H, T2])
        cT = qcT
        hT = qcT[:, 0:FC, :]
        raw = sb("raw", [S, RAWS, S2])
        prob = sb("prob", [KR, PROBS, G * S])
        probT = sb("probT", [KR, 2, KJ, G * S])
        negmax = sb("negmax", [P, G * SG + NH])
        total = sb("total", [P, G * SG + NH])
        rtotal = sb("rtotal", [P, G * SG + NH])
        smask = sb("smask", [S, NB, S], i32)
        smask0 = sb("smask0", [S, NB, S], i32)
        cmask = sb("cmask", [P, NB, S2], i32)
        cbias = sb("cbias", [S, NB, S2])
        FW = 2 * EK * E + 2 * E
        q_flat = qcT[:, :, :].rearrange("p h t -> p (h t)")
        fw = [q_flat[:, 0:FW], q_flat[:, FW:2 * FW], oT[:, :, :].rearrange("p c t -> p (c t)")[:, 0:FW]]
        fwq = [a[:, 0:EK * E].rearrange("p (k n) -> p k n", k=EK) for a in fw]
        fwo = [a[:, EK * E:2 * EK * E].rearrange("p (k n) -> p k n", k=EK) for a in fw]
        fwk = [a[:, 2 * EK * E:2 * EK * E + E] for a in fw]
        fwv = [a[:, 2 * EK * E + E:FW] for a in fw]
        fkT = v_all[:, 0:NB * EK * S2].rearrange("p (b k n) -> p b k n", b=NB, k=EK)
        fqT = v_all[:, NB * EK * S2:NB * EK * S2 + EK * T2].rearrange("p (k n) -> p k n", k=EK)
        fcT = sb("fcT", [P, T2])
        faT = tnT_next
        fcol = sb("fcol", [P, 3, 3, EK])
        fbias = prob[:, PROBS - 3:PROBS, :].rearrange("p a n -> p (a n)")[:, 0:5 * E].rearrange("p (a n) -> p a n", a=5)

        banks = {n: scope.enter_context(nc.psum_tensor(n, [P, 512], f32))
                 for n in ("proj0", "proj1", "score0", "score1", "tr0", "tr1", "sum0", "sum1")}
        ready = {n: sem(f"{n}_ready") for n in banks}
        taken = {n: sem(f"{n}_taken") for n in banks if "score" not in n}

        setup_ids = sem("setup_ids")
        setup_done = sem("setup_done")
        front_loaded = sem("front_loaded")
        x_loaded = sem("x_loaded")
        ctx_loaded = sem("ctx_loaded")
        smask_loaded = sem("smask_loaded")
        cmask_loaded = sem("cmask_loaded")
        smask_used = sem("smask_used")
        cmask_used = sem("cmask_used")
        front_done = sem("front_done")
        loaded = {n: sem(f"{n}_loaded") for n in
                  ("w_q", "w_kv", "w_o", "c_q", "c_kT", "c_v", "c_o", "f_1", "f_2", "small")}
        dve_step = sem("dve_step")
        pool_step = sem("pool_step")
        passed = sem("passed")
        stats_ready = sem("stats_ready")
        rstd_ready = sem("rstd_ready")
        tn_ready = sem("tn_ready")
        resid_ready = sem("resid_ready")
        negmax_ready = sem("negmax_ready")
        exp_ready = sem("exp_ready")
        rtotal_ready = sem("rtotal_ready")
        prob_ready = sem("prob_ready")
        stored = sem("stored")

        SMALL = 6
        FRONT_DMAS = 3 * 6 + 2 + 1 + 5 + 2

        block = scope.enter_context(nc.Block())

        @block.sync
        def _(sp):
            def spread(a, rows):
                return a.partition_broadcast(rows)

            def load_pair_x(p):
                sp.dma_start(tw[:, :, :], x[ds(p * NB, NB)].rearrange("b s e -> s b e")).then_inc(x_loaded, 16)
                sp.dma_start(cmask[:, :, :], ctx_mask[ds(p * NB, NB)].partition_broadcast(P)).then_inc(x_loaded, 16)

            def load_pair_ctx(p):
                sp.dma_start(ctxN[:, :, :, :], ctx_nat[ds(p * NB, NB)].rearrange("b (j r) c -> r b j c", r=KR))\
                    .then_inc(ctx_loaded, 16)

            def load_pair_smask(p):
                sp.dma_start(smask[:, :, :], self_mask[ds(p * NB, NB)].rearrange("b q k -> q b k")).then_inc(smask_loaded, 16)

            def load_pair_cmask(p):
                sp.dma_start(cmask[:, :, :], ctx_mask[ds(p * NB, NB)].partition_broadcast(P)).then_inc(cmask_loaded, 16)

            def chunks(a, l):
                return a[ds(l, 1)].rearrange("o (k p) n -> p (o k) n", p=P)

            def load_qkv(l):
                sp.dma_start(w_q[:, :, :], chunks(dec["sa_q"], l)).then_inc(loaded["w_q"], 16)
                sp.dma_start(w_kv[:, :, :], chunks(dec["sa_kv"], l)).then_inc(loaded["w_kv"], 16)

            def load_w_o(l):
                sp.dma_start(w_o[:, :, :], chunks(dec["sa_ow"], l)).then_inc(loaded["w_o"], 16)

            def load_ca(l):
                sp.dma_start(c_q[:, :, :], chunks(dec["ca_q"], l)).then_inc(loaded["c_q"], 16)
                sp.dma_start(c_kT[:, :, :], chunks(dec["ca_kT"], l)).then_inc(loaded["c_kT"], 16)
                values = dec["ca_kv"][ds(l, 1), :, HDIM:2 * HDIM].rearrange("o c (h t d) -> c (o h) t d", t=2, d=D)
                for half in range(2):
                    sp.dma_start(c_v[:, half::2, half, :], values[:, :, half, :]).then_inc(loaded["c_v"], 16)
                sp.dma_start(c_o[:, :, :], chunks(dec["ca_ow"], l)).then_inc(loaded["c_o"], 16)

            def load_ff(l):
                sp.dma_start(f_1[:, :, :], chunks(dec["ff_w1"], l)).then_inc(loaded["f_1"], 16)
                sp.dma_start(f_2[:, :, :], chunks(dec["ff_w2"], l)).then_inc(loaded["f_2"], 16)

            def load_small(l):
                sp.dma_start(f_b1[:, :], dec["ff_b1"][ds(l, 1)].rearrange("o p k -> p (o k)")).then_inc(loaded["small"], 16)
                for n, name in enumerate(("pre_g", "pre_b")):
                    sp.dma_start(pre[:, n, :], dec[name][ds(l, 1)].rearrange("o p k -> p (o k)"))\
                        .then_inc(loaded["small"], 16)
                for n, name in enumerate(("sa_ob", "ca_ob", "ff_b2")):
                    sp.dma_start(o_bias[:, n, :], dec[name][ds(l, 1)].partition_broadcast(S)).then_inc(loaded["small"], 16)

            load_pair_x(0)
            for n in range(3):
                sp.dma_start(fwq[n], front[n]["Wq"].rearrange("(k p) n -> p k n", p=P)).then_inc(front_loaded, 16)
                sp.dma_start(fwk[n], front[n]["Wk"]).then_inc(front_loaded, 16)
                for j, name in enumerate(("bq", "bk", "bv")):
                    sp.dma_start(fcol[:, n, j, :], front[n][name]).then_inc(front_loaded, 16)
                if n == 0:
                    sp.dma_start(ctxT[:, :], ctx_tr).then_inc(front_loaded, 16)
                    load_pair_ctx(0)
                sp.dma_start(fwv[n], front[n]["Wv"]).then_inc(front_loaded, 16)
                if n != 1:
                    sp.dma_start(fwo[n], front[n]["Wo"].rearrange("(k p) n -> p k n", p=P)).then_inc(front_loaded, 16)
            for n, a in enumerate((front[0]["bo"], front[2]["bo"], front[1]["bv_row"], front[1]["gamma"], front[1]["beta"])):
                sp.dma_start(fbias[:, n, :], spread(a, KR)).then_inc(front_loaded, 16)
            for n, name in enumerate(("norm_g", "norm_b")):
                sp.dma_start(norm[:, n, :], dec[name]).then_inc(front_loaded, 16)
            load_qkv(0)
            load_w_o(0)
            sp.wait_ge(setup_done, 1)
            load_ca(0)
            load_ff(0)
            load_small(0)
            with sp.Fori(1, PAIRS) as p:
                sp.wait_ge(front_done, p)
                load_pair_x(p)
                load_pair_ctx(p)
            sp.wait_ge(front_done, PAIRS)
            load_pair_ctx(0)
            load_pair_smask(0)
            load_pair_cmask(0)

            def next_pair(at, p):
                sp.wait_ge(smask_used, at.it + 1)
                load_pair_smask(p)
                sp.wait_ge(cmask_used, at.it + 1)
                load_pair_cmask(p)
                sp.wait_ge(ready["proj1"], at.at("proj1", CA_OUT + 1))
                load_pair_ctx(p)

            def layer(l, last):
                with sp.Fori(1, PAIRS) as p:
                    next_pair(Place(MAIN_LOOP, l * PAIRS + p - 1), p)
                at = Place(MAIN_LOOP, l * PAIRS + PAIRS - 2)
                sp.wait_ge(ready["proj1"], at.at("proj1", Q_END))
                if last:
                    sp.wait_ge(smask_used, L * PAIRS)
                    load_pair_smask(0)
                    sp.sem_inc(loaded["w_q"], 16)
                    sp.sem_inc(loaded["w_kv"], 16)
                    return
                load_qkv(l + 1)
                at = Place(MAIN_LOOP, l * PAIRS + PAIRS - 1)
                sp.wait_ge(ready["proj1"], at.at("proj1", SA_OUT + 1))
                load_w_o(l + 1)
                next_pair(at, 0)
                load_ca(l + 1)
                sp.wait_ge(taken["proj1"], at.emptied("proj1", FF_OUT + 1))
                load_small(l + 1)
                load_ff(l + 1)

            with sp.Fori(0, L - 1) as l:
                layer(l, False)
            layer(L - 1, True)
            sp.wait_ge(taken["proj1"], Place(MAIN_LOOP, L * PAIRS).emptied("proj1", 0))
            sp.dma_start(out.rearrange("b s e -> s b e"), t_all[:, :, :]).then_inc(stored, 16)
            sp.wait_ge(stored, 16)

        @block.gpsimd
        def _(pool):
            pool.memset(ident[:, :], 0.0).then_inc(setup_ids, 1)
            pool.memset(eps[:, 0, :], 1e-5)
            pool.memset(eps[:, 1, :], 1e-6)
            pool.memset(minus_half[:, :], -0.5)
            pool.memset(masked[:, :], MASKED)
            pool.memset(cbias[:, :, :], 0.0)
            pool.memset(c_v[:, :, :, :], 0.0)
            pool.memset(k_diag[:, :, :, :], 0.0).then_inc(setup_ids, 1)
            pool.wait_ge(setup_ids, 2)
            pool.affine_select(out=ident[:, :], in_=ident[:, :], compare_op=ALU.not_equal, fill=1.0, base=0,
                               pattern=[[-1, P]], channel_multiplier=1).then_inc(setup_done, 1)
            for name in taken:
                pool.sem_inc(taken[name], 1)

            def inverse_std(at, which):
                k = at.next("stats")
                pool.wait_ge(stats_ready, at.at("stats", k + 1))
                pool.tensor_tensor(veps[:, :], mv[:, :, 1], eps[:, which, :], ALU.add).then_inc(pool_step, 1)
                pool.wait_ge(pool_step, at.at("pool", at.next("pool") + 1))
                pool.tensor_tensor(rstd[:, :], veps[:, :], minus_half[:, :], ALU.pow).then_inc(rstd_ready, 1)

            def add_bias(bias):
                pool.tensor_tensor(tw[:, :, :], tw[:, :, :], bias.unsqueeze(1).broadcast_to([S, NB, E]), ALU.add)\
                    .then_inc(resid_ready, 1)

            pool.wait_ge(front_loaded, 16 * FRONT_DMAS)
            with pool.Fori(0, PAIRS) as p:
                at = Place(FRONT_LOOP, p)
                pool.wait_ge(ready["proj0"], at.at("proj0", 1))
                add_bias(fbias[0:S, 0, :])
                inverse_std(at, 1)
                pool.wait_ge(ready["proj0"], at.at("proj0", 10))
                add_bias(fbias[0:S, 1, :])

            def normalise_group(at, g):
                pr = prob[0:S, g % PROBS, :].rearrange("p (h k) -> p h k", h=G)
                pool.wait_ge(rtotal_ready, at.at("rtotal", g + 1))
                pool.tensor_tensor(pr, pr, rtotal[0:S, G * g:G * g + G].unsqueeze(2).broadcast_to([S, G, S]), ALU.mult)\
                    .then_inc(prob_ready, 1)

            inverse_std(Place(START), 0)
            for g in range(EARLY - 1):
                normalise_group(Place(MAIN_LOOP), g)
            with pool.Fori(0, L) as l:
                with pool.Fori(0, PAIRS) as p:
                    at = Place(MAIN_LOOP, l * PAIRS + p)
                    pool.wait_ge(loaded["small"], (l + 1) * (16 * SMALL))
                    pool.wait_ge(taken["proj1"], at.emptied("proj1", 0))
                    pool.tensor_tensor(tw[:, :, :], t_all[:, ds(p * NB, NB), :],
                                       o_bias[:, 0, :].unsqueeze(1).broadcast_to([S, NB, E]), ALU.add).then_inc(resid_ready, 1)
                    for g in range(EARLY - 1, SG):
                        normalise_group(at, g)
                    inverse_std(at, 0)
                    for n in (1, 2):
                        inverse_std(at, 0)
                        pool.wait_ge(tn_ready, at.at("tn", NB * (n + 1)))
                        add_bias(o_bias[:, n, :])
                        if n == 1:
                            for i in range(NH):
                                row = prob[0:S, i % PROBS, 0:S2]
                                pool.wait_ge(rtotal_ready, at.at("rtotal", SG + i + 1))
                                pool.tensor_tensor(row, row, rtotal[0:S, G * SG + i:G * SG + i + 1].broadcast_to([S, S2]),
                                                   ALU.mult).then_inc(prob_ready, 1)
                    for g in range(EARLY - 1):
                        normalise_group(Place(MAIN_LOOP, l * PAIRS + p + 1), g)
                    at.check()

        @block.tensor
        def _(pe):
            def fill(at, name):
                if name in taken:
                    pe.wait_ge(taken[name], at.emptied(name, at.next(name)))
                return banks[name]

            def done(ins, name):
                ins.then_inc(ready[name], 1)

            def transposes_of(at, a, name="proj0"):
                bank = fill(at, name)
                for k in range(EK):
                    for b in range(NB):
                        ins = pe.transpose(bank[:, k * T2 + b * S:k * T2 + (b + 1) * S], a[:, b, k * P:(k + 1) * P],
                                           ident[0:S, 0:S])
                done(ins, name)

            def project(at, name, weights, moving):
                bank = fill(at, name)
                for k, (w, m) in enumerate(zip(weights, moving)):
                    ins = pe.matmul(bank[0:w.shape[1], 0:m.shape[1]], w, m, start=k == 0, stop=k == len(weights) - 1)
                done(ins, name)

            def out_rows(at, stationary, weights, written=False, slots=("proj1",), between=None):
                counts = dict(at.n)
                for b in range(NB):
                    if between and b == 1:
                        between()
                    if b < len(slots):
                        bank, col = fill(at, slots[b]), 0
                    else:
                        col = b * E
                    terms = [(a[:, b * S:(b + 1) * S], w) for a, w in zip(stationary, weights)]
                    for k, (a, w) in enumerate(terms):
                        if written and b == 0:
                            name, fills = f"proj{k % 2}", len(terms) // 2
                            pe.wait_ge(taken[name], at.emptied(name, counts[name] - fills + k // 2 + 1))
                        ins = pe.matmul(bank[0:S, col:col + E], a, w, start=k == 0, stop=k == len(terms) - 1)
                    if b >= NB - len(slots):
                        done(ins, slots[b - NB + len(slots)])

            pe.wait_ge(setup_done, 1)
            pe.wait_ge(front_loaded, 16 * FRONT_DMAS)
            with pe.Fori(0, PAIRS) as p:
                at = Place(FRONT_LOOP, p)
                pe.wait_ge(x_loaded, (p + 1) * 32)
                pe.wait_ge(ctx_loaded, (p + 1) * 16)
                for n in range(3):
                    if n == 1:
                        pe.wait_ge(taken["proj1"], at.emptied("proj1", at.n["proj1"]))
                    if n == 2:
                        pe.wait_ge(tn_ready, p + 1)
                    transposes_of(at, tw)
                    pe.wait_ge(taken["proj0"], at.emptied("proj0", at.n["proj0"]))
                    for e in range(EK):
                        project(at, f"proj{e}", [fwq[n][:, k, e * P:(e + 1) * P] for k in range(EK)],
                                [tnT[:, k, :] for k in range(EK)])
                    for b in range(NB):
                        for e in range(EK):
                            project(at, f"proj{e}", [fwk[n][:, e * P:(e + 1) * P]], [ctxT[:, ds(p * (NB * S2) + b * S2, S2)]])
                    for b in range(NB):
                        for e in range(EK):
                            pe.wait_ge(taken[f"proj{e}"], at.emptied(f"proj{e}", at.n[f"proj{e}"] - (NB - 1 - b)))
                        name = f"score{b}"
                        if n == 1:
                            pe.wait_ge(negmax_ready, at.at("negmax", b + 1))
                        elif n == 2:
                            pe.wait_ge(exp_ready, at.at("exp", NB + b + 1))
                        if n != 1:
                            project(at, name, [fqT[:, e, b * S:(b + 1) * S] for e in range(EK)],
                                    [fkT[:, b, e, :] for e in range(EK)])
                        else:
                            bank = banks[name]
                            for j in range(KJ):
                                for e in range(EK):
                                    ins = pe.matmul(bank[0:KR, j * S:(j + 1) * S], fkT[:, b, e, j * KR:(j + 1) * KR],
                                                    fqT[:, e, b * S:(b + 1) * S], start=e == 0, stop=e == EK - 1)
                            done(ins, name)
                    if n != 1:
                        for b in range(NB):
                            name = f"tr{b}"
                            pe.wait_ge(prob_ready, at.at("prob", NB * n + b + 1))
                            bank = fill(at, name)
                            for j in range(KJ):
                                ins = pe.transpose(bank[0:KR, j * S:(j + 1) * S], prob[0:S, b, j * KR:(j + 1) * KR],
                                                   ident[0:S, 0:S])
                            done(ins, name)
                    for b in range(NB):
                        if n != 1:
                            pe.wait_ge(taken[f"tr{b}"], at.emptied(f"tr{b}", at.n[f"tr{b}"]))
                        else:
                            pe.wait_ge(prob_ready, at.at("prob", NB * n + b + 1))
                        project(at, f"sum{b}", [ctxN[:, b, j, :] for j in range(KJ)],
                                [probT[:, b, j, 0:S] for j in range(KJ)])
                    for b in range(NB):
                        pe.wait_ge(taken[f"sum{b}"], at.emptied(f"sum{b}", at.n[f"sum{b}"]))
                    if n != 1:
                        for e in range(EK):
                            project(at, f"proj{e}", [fwv[n][:, e * P:(e + 1) * P]], [fcT[:, :]])
                        for e in range(EK):
                            pe.wait_ge(taken[f"proj{e}"], at.emptied(f"proj{e}", at.n[f"proj{e}"]))
                        out_rows(at, [faT[:, e, :] for e in range(EK)], [fwo[n][:, e, :] for e in range(EK)])
                    else:
                        bank = fill(at, "proj1")
                        for b in range(NB):
                            o = bank[0:S, b * E:(b + 1) * E]
                            pe.matmul(o, fcT[:, b * S:(b + 1) * S], fwv[n], start=True, stop=False)
                            for j in range(KJ):
                                ins = pe.matmul(o, probT[:, b, j, 0:S], fbias[0:KR, 2, :], start=False, stop=j == KJ - 1)
                        done(ins, "proj1")
                at.check()
            pe.wait_ge(front_done, PAIRS)


            def normed(at, n, name):
                pe.wait_ge(tn_ready, at.at("tn", NB * (n + 1)))
                transposes_of(at, tn, name)

            def projected(at, name, w, m, c):
                project(at, name, [w[:, k, c * P:(c + 1) * P] for k in range(EK)], [m[:, k, :] for k in range(EK)])

            def chunked(at, w, m, chunks):
                for c in chunks:
                    projected(at, f"proj{c % 2}", w, m, c)

            def emptied(at, *names):
                for name in names:
                    pe.wait_ge(taken[name], at.emptied(name, at.n[name]))

            def values(at, banks_of_values):
                for i in banks_of_values:
                    b, n = i // V2, i % V2
                    col = HDIM + n * 512
                    project(at, f"proj{n % 2}", [tnT_next[:, k, b * S:(b + 1) * S] for k in range(EK)],
                            [w_kv[:, k, col:col + 512] for k in range(EK)])

            OUT_SLOTS = ("sum1", "proj1")

            def self_scores(at, t):
                b, c = t // GB, t % GB * 2
                if t < 2:
                    pe.wait_ge(negmax_ready, at.base("negmax"))
                else:
                    pe.wait_ge(exp_ready, at.at("exp", t - 1))
                bank = banks[f"score{t % 2}"]
                for n in range(2):
                    ins = pe.matmul(bank[0:S, n * T2:(n + 1) * T2], qT[:, c + n, b * S:(b + 1) * S],
                                    k_diag[:, c + n, :, b * S:(b + 1) * S], start=True, stop=True)
                done(ins, f"score{t % 2}")

            at = Place(START)
            normed(at, 0, "proj0")
            emptied(at, "proj0")
            pe.wait_ge(loaded["w_kv"], 16)
            values(at, range(NB * V2))
            pe.wait_ge(loaded["w_q"], 16)
            chunked(at, w_q, tnT_next, range(HC))
            chunked(at, w_kv, tnT_next, range(HC))
            at.check()
            emptied(at, "proj0", "proj1")
            for t in range(EARLY):
                self_scores(Place(MAIN_LOOP), t)

            with pe.Fori(0, L) as l:
                with pe.Fori(0, PAIRS) as p:
                    it = l * PAIRS + p
                    next_layer = (it + 1) // PAIRS
                    at = Place(MAIN_LOOP, it)

                    def weights(name):
                        pe.wait_ge(loaded[name], (l + 1) * (32 if name == "c_v" else 16))

                    for n in range(2):
                        pe.wait_ge(taken[f"proj{n}"], at.emptied(f"proj{n}", 0))
                    for t in range(EARLY, SG + SA_LAG + SUM_LAG):
                        if t < SG:
                            self_scores(at, t)
                        if 0 <= t - SA_LAG - SUM_LAG < SG:
                            g = t - SA_LAG - SUM_LAG
                            b, c = g // GB, g % GB * 2
                            pe.wait_ge(taken[f"tr{g % 2}"], at.emptied(f"tr{g % 2}", g // 2 + 1))
                            bank = fill(at, f"sum{g % 2}")
                            for n in range(2):
                                ins = pe.matmul(bank[:, n * T2:(n + 1) * T2], v[:, b, (c + n) * P:(c + n + 1) * P],
                                                probT[0:S, g % 2, 0, n * T2:(n + 1) * T2], start=True, stop=True)
                            done(ins, f"sum{g % 2}")
                        if 0 <= t - SA_LAG < SG:
                            g = t - SA_LAG
                            pe.wait_ge(prob_ready, at.at("prob", g + 1))
                            bank = fill(at, f"tr{g % 2}")
                            for h in range(G):
                                ins = pe.transpose(bank[0:S, h * S:(h + 1) * S], prob[0:S, g % PROBS, h * S:(h + 1) * S],
                                                   ident[0:S, 0:S])
                            done(ins, f"tr{g % 2}")
                    emptied(at, "sum0", "sum1")
                    normed(at, 0, "proj0")
                    weights("w_o")
                    out_rows(at, [oT[:, c, :] for c in range(HC)], [w_o[:, c, :] for c in range(HC)], slots=OUT_SLOTS)
                    emptied(at, "proj0")
                    pe.wait_ge(loaded["w_kv"], (next_layer + 1) * 16)
                    values(at, range(NB * V2 - 1))

                    normed(at, 1, "sum0")
                    values(at, range(NB * V2 - 1, NB * V2))
                    weights("c_q")
                    emptied(at, "sum0")
                    weights("c_kT")
                    for n in range(HC + 2):
                        if n < HC:
                            projected(at, f"sum{n % 2}", c_q, tnT, n)
                        if n >= 2:
                            c = n - 2
                            slot = f"sum{c % 2}"
                            pe.wait_ge(taken[slot], at.emptied(slot, (SUM_Q + c) // 2 + 1))
                            project(at, f"proj{c % 2}", [c_kT[:, c, :]], [q_diag[:, c, :, :].rearrange("p h t -> p (h t)")])
                    fills = dict(at.n)
                    pe.wait_ge(ctx_loaded, (it + PAIRS + 1) * 16)
                    for t in range(NH + CA_LAG + SUM_LAG):
                        if t < NH:
                            b, h = t // H, t % H
                            if b == 0 and h % 2 == 0:
                                name = f"proj{h // 2 % 2}"
                                pe.wait_ge(taken[name], at.emptied(name, fills[name] - HC // 2 + h // 4 + 1))
                            if t < 2:
                                pe.wait_ge(exp_ready, at.at("exp", SG))
                            else:
                                pe.wait_ge(negmax_ready, at.at("negmax", SG + t - 1))
                            project(at, f"score{t % 2}", [qcT[:, h, b * S:(b + 1) * S]],
                                    [ctxT[:, ds(p * (NB * S2) + b * S2, S2)]])
                        if t in KEY_STEPS:
                            c = KEY_STEPS[t]
                            projected(at, f"proj{c % 2}", w_kv, tnT_next, c)
                        if 0 <= t - CA_LAG < NH:
                            i = t - CA_LAG
                            pe.wait_ge(prob_ready, at.at("prob", SG + i + 1))
                            bank = fill(at, f"tr{i % 2}")
                            for j in range(KJ):
                                ins = pe.transpose(bank[0:KR, j * S:(j + 1) * S], prob[0:S, i % PROBS, j * KR:(j + 1) * KR],
                                                   ident[0:S, 0:S])
                            done(ins, f"tr{i % 2}")
                        if 0 <= t - CA_LAG - SUM_LAG < NH and (t - CA_LAG - SUM_LAG) % G == G - 1:
                            g = (t - CA_LAG - SUM_LAG) // G
                            b = g // GB
                            for i in range(2):
                                pe.wait_ge(taken[f"tr{i}"], at.emptied(f"tr{i}", (SG + G * (g + 1)) // 2))
                            project(at, f"sum{g % 2}", [ctxN[:, b, j, :] for j in range(KJ)],
                                    [probT[:, g % 2, j, :] for j in range(KJ)])
                    weights("c_v")
                    for c in range(HC):
                        if c % 2 == 0:
                            g = SUM_CA + GB + c // 2
                            pe.wait_ge(taken[f"sum{g % 2}"], at.emptied(f"sum{g % 2}", g // 2 + 1))
                        project(at, f"proj{c % 2}", [c_v[:, 2 * c + n, :, :].rearrange("p t d -> p (t d)") for n in range(2)],
                                [cT[:, 2 * c + n, :] for n in range(2)])
                    weights("c_o")
                    out_rows(at, [oT[:, c, :] for c in range(HC)], [c_o[:, c, :] for c in range(HC)], written=True,
                             slots=OUT_SLOTS)
                    pe.wait_ge(loaded["w_q"], (next_layer + 1) * 16)
                    chunked(at, w_q, tnT_next, range(HC - 1))

                    normed(at, 2, "sum0")
                    chunked(at, w_q, tnT_next, range(HC - 1, HC))
                    fills = dict(at.n)
                    weights("f_1")
                    emptied(at, "sum0")
                    chunked(at, f_1, tnT, range(FC))
                    for name in ("proj0", "proj1"):
                        pe.wait_ge(taken[name], at.emptied(name, fills[name]))
                    for t in range(EARLY - 1):
                        self_scores(Place(MAIN_LOOP, it + 1), t)
                    weights("f_2")
                    out_rows(at, [hT[:, c, :] for c in range(FC)], [f_2[:, c, :] for c in range(FC)], written=True,
                             slots=OUT_SLOTS, between=lambda: self_scores(Place(MAIN_LOOP, it + 1), EARLY - 1))
                    at.check()

        @block.scalar
        def _(act):
            def filled(at, name):
                act.wait_ge(ready[name], at.at(name, at.next(name) + 1))
                return banks[name]

            def copy(o, i):
                return act.activation(o, i, ACT.Copy)

            def plus(o, i, bias):
                return act.activation(o, i, ACT.Identity, bias=bias)

            def softmax_row(at, k, o, i, scale, col):
                act.wait_ge(negmax_ready, at.at("negmax", k + 1))
                act.activation(o, i, ACT.Exp, bias=negmax[0:S, col:col + 1], scale=scale,
                               accum_out=total[0:S, col:col + 1]).then_inc(exp_ready, 1)

            act.wait_ge(setup_done, 1)
            act.wait_ge(front_loaded, 16 * FRONT_DMAS)
            with act.Fori(0, PAIRS) as p:
                at = Place(FRONT_LOOP, p)
                for n in range(3):
                    bank = filled(at, "proj0")
                    copy(tnT[:, :, :].rearrange("p k t -> p (k t)"), bank[:, 0:EK * T2]).then_inc(taken["proj0"], 1)
                    bank = filled(at, "proj0")
                    plus(fqT[:, 0, :], bank[:, 0:T2], fcol[:, n, 0, 0:1]).then_inc(taken["proj0"], 1)
                    for b in range(NB):
                        bank = filled(at, "proj0")
                        plus(fkT[:, b, 0, :], bank[:, 0:S2], fcol[:, n, 1, 0:1]).then_inc(taken["proj0"], 1)
                    for b in range(NB):
                        if n != 1:
                            softmax_row(at, NB * n + b, prob[0:S, b, 0:S2], raw[:, b, :], -1.0, b)
                        else:
                            bank = banks[f"score{b}"]
                            act.wait_ge(negmax_ready, at.at("negmax", NB * n + b + 1))
                            for j in range(KJ):
                                ins = act.activation(prob[0:KR, b, j * S:(j + 1) * S], bank[0:KR, j * S:(j + 1) * S],
                                                     ACT.Exp, bias=negmax[0:KR, NB + KJ * b + j:NB + KJ * b + j + 1],
                                                     scale=FRONT_SCALE,
                                                     accum_out=total[0:KR, NB + KJ * b + j:NB + KJ * b + j + 1])
                            ins.then_inc(exp_ready, 1)
                    if n != 1:
                        bank = filled(at, "tr0")
                        copy(probT[:, 0, :, 0:S], bank[0:KR, 0:KJ * S].rearrange("p (j s) -> p j s", j=KJ))\
                            .then_inc(taken["tr0"], 1)
                    bank = filled(at, "sum0")
                    copy(fcT[:, 0:S], bank[:, 0:S]).then_inc(taken["sum0"], 1)
                    if n != 1:
                        bank = filled(at, "proj0")
                        plus(faT[:, 0, :], bank[:, 0:T2], fcol[:, n, 2, 0:1]).then_inc(taken["proj0"], 1)


            def normed(at, o, scale_bias, name):
                bank = filled(at, name)
                for k in range(EK):
                    ins = act.activation(o[:, k, :], bank[:, k * T2:(k + 1) * T2], ACT.Identity,
                                         scale=scale_bias[:, 0, k:k + 1], bias=scale_bias[:, 1, k:k + 1])
                ins.then_inc(taken[name], 1)

            def self_exponentials(at, t):
                act.wait_ge(ready[f"tr{t % 2}"], at.at(f"tr{t % 2}", t // 2 - PROBS // 2 + 1))
                act.wait_ge(negmax_ready, at.at("negmax", t + 1))
                bank = banks[f"score{t % 2}"]
                for h in range(G):
                    col = G * t + h
                    ins = act.activation(prob[0:S, t % PROBS, h * S:(h + 1) * S], bank[0:S, h * S:(h + 1) * S],
                                         ACT.Exp, bias=negmax[0:S, col:col + 1], scale=SCALE,
                                         accum_out=total[0:S, col:col + 1])
                ins.then_inc(exp_ready, 1)

            def diagonal(at, name, o, c):
                bank = filled(at, name)
                for h in range(2):
                    ins = copy(o[h * D:(h + 1) * D, c, h, :], bank[h * D:(h + 1) * D, 0:T2])
                ins.then_inc(taken[name], 1)

            def chunk(at, o, n, func=ACT.Copy, **kw):
                bank = filled(at, "proj0")
                act.activation(o, bank[0:o.shape[0], 0:n], func, **kw).then_inc(taken["proj0"], 1)

            def values(at):
                for b in range(NB):
                    chunk(at, v[:, b, 0:512], 512)

            def queries(at):
                for c in range(0, HC, 2):
                    chunk(at, qT[:, c, :], T2)

            at = Place(START)
            normed(at, tnT_next, norm, "proj0")
            values(at)
            queries(at)
            for c in range(0, HC, 2):
                diagonal(at, "proj0", k_diag, c)
            at.check()
            for t in range(EARLY):
                self_exponentials(Place(MAIN_LOOP), t)
            with act.Fori(0, L) as l:
                with act.Fori(0, PAIRS) as p:
                    at = Place(MAIN_LOOP, l * PAIRS + p)

                    for t in range(EARLY, SG + SA_LAG + SUM_LAG):
                        if 0 <= t - SA_LAG - SUM_LAG < SG and (t - SA_LAG - SUM_LAG) % 2 == 0:
                            b, c = (t - SA_LAG - SUM_LAG) // GB, (t - SA_LAG - SUM_LAG) % GB * 2
                            bank = filled(at, "sum0")
                            for h in range(2):
                                r = slice(h * D, (h + 1) * D)
                                ins = copy(oT[r, c:c + 2, b * S:(b + 1) * S],
                                           bank[r, 0:2 * T2].rearrange("p (n h s) -> p n h s", n=2, h=2)[:, :, h, :])
                            ins.then_inc(taken["sum0"], 1)
                        if 0 <= t - SA_LAG < SG and (t - SA_LAG) % 2 == 0:
                            bank = filled(at, "tr0")
                            copy(probT[0:S, 0, 0, :], bank[0:S, 0:G * S]).then_inc(taken["tr0"], 1)
                        if t < SG:
                            self_exponentials(at, t)

                    normed(at, tnT_next, norm, "proj0")
                    values(at)
                    normed(at, tnT, norm, "sum0")
                    for n in range(0, HC + 2, 2):
                        if n < HC:
                            diagonal(at, "sum0", q_diag, n)
                        if n >= 2:
                            chunk(at, qcT[:, 2 * n - 4:2 * n - 2, :].rearrange("p h t -> p (h t)"), 2 * T2)
                    for t in range(NH + CA_LAG + SUM_LAG):
                        if 0 <= t - CA_LAG < NH and (t - CA_LAG) % 2 == 0:
                            i = t - CA_LAG
                            if i % G == 0:
                                g = SUM_CA + i // G
                                act.wait_ge(ready[f"sum{g % 2}"], at.at(f"sum{g % 2}", g // 2))
                            bank = filled(at, "tr0")
                            copy(probT[:, i // G % 2, :, i % G * S:(i % G + 1) * S],
                                 bank[0:KR, 0:KJ * S].rearrange("p (j s) -> p j s", j=KJ)).then_inc(taken["tr0"], 1)
                        if t < NH:
                            k = SG + t
                            act.wait_ge(ready[f"tr{t % 2}"], at.at(f"tr{t % 2}", k // 2 - PROBS // 2 + 1))
                            softmax_row(at, k, prob[0:S, t % PROBS, 0:S2], raw[:, t % RAWS, :], -1.0, G * SG + t)
                        if 0 <= t - CA_LAG - SUM_LAG < NH and (t - CA_LAG - SUM_LAG) % (2 * G) == G - 1:
                            g = (t - CA_LAG - SUM_LAG) // G
                            b, h = g // GB, g % GB * G
                            bank = filled(at, "sum0")
                            copy(cT[:, h:h + G, b * S:(b + 1) * S], bank[:, 0:G * S].rearrange("p (h s) -> p h s", h=G))\
                                .then_inc(taken["sum0"], 1)
                        if KEY_STEPS.get(t, 1) % 2 == 0:
                            diagonal(at, "proj0", k_diag, KEY_STEPS[t])
                    for c in range(0, HC, 2):
                        chunk(at, oT[:, c, :], T2)
                    queries(at)
                    act.wait_ge(loaded["small"], (l + 1) * (16 * SMALL))
                    normed(at, tnT, pre, "sum0")
                    early = Place(MAIN_LOOP, l * PAIRS + p + 1)
                    for c in range(0, FC, 2):
                        chunk(at, hT[:, c, :], T2, ACT.Relu, bias=f_b1[:, c:c + 1])
                    for t in range(EARLY):
                        self_exponentials(early, t)
                    assert at.n["proj0"] == MAIN["proj0"] and at.n["tr0"] == MAIN["tr0"] and at.n["sum0"] == MAIN["sum0"]

        @block.vector
        def _(dve):
            def filled(at, name):
                dve.wait_ge(ready[name], at.at(name, at.next(name) + 1))
                return banks[name]

            def gate(s, value):
                dve.wait_ge(s, value)
                dve.sem_inc(passed, 1)

            def link(at, ins):
                ins.then_inc(dve_step, 1)
                linked(at)

            def linked(at):
                gate(dve_step, at.at("dve", at.next("dve") + 1))

            def plus(o, i, bias):
                return dve.tensor_scalar(o, i, bias, None, ALU.add)

            def statistics(at, a):
                for b in range(NB):
                    ins = dve.bn_stats(stats[:, b, :], a[:, b, :])
                variances(at, ins)

            def variances(at, ins):
                link(at, ins)
                for b in range(NB):
                    ins = dve.bn_aggr(mv[:, b, :], stats[:, b, :])
                ins.then_inc(stats_ready, 1)

            def wait_rstd(at):
                dve.wait_ge(rstd_ready, at.at("stats", at.next("stats") + 1))

            def normalise(o, a, b):
                return dve.tensor_scalar(o, a[:, b, :], mv[:, b, 0:1], rstd[:, b:b + 1], ALU.subtract, ALU.mult)

            dve.wait_ge(setup_done, 1)
            dve.wait_ge(front_loaded, 16 * FRONT_DMAS)
            with dve.Fori(0, PAIRS) as p:
                at = Place(FRONT_LOOP, p)
                dve.wait_ge(x_loaded, (p + 1) * 32)
                for n in range(3):
                    bank = filled(at, "proj1")
                    plus(fqT[:, 1, :], bank[:, 0:T2], fcol[:, n, 0, 1:2]).then_inc(taken["proj1"], 1)
                    for b in range(NB):
                        bank = filled(at, "proj1")
                        plus(fkT[:, b, 1, :], bank[:, 0:S2], fcol[:, n, 1, 1:2]).then_inc(taken["proj1"], 1)
                    for b in range(NB):
                        if n != 1:
                            k = at.next(f"score{b}")
                            gate(ready[f"score{b}"], at.at(f"score{b}", k + 1))
                            dve.tensor_tensor_reduce(out=raw[:, b, :], in0=banks[f"score{b}"][0:S, 0:S2], in1=cbias[:, b, :],
                                                     scale=-FRONT_SCALE, scalar=3.4e38, op0=ALU.add, op1=ALU.min,
                                                     accum_out=negmax[0:S, b:b + 1]).then_inc(negmax_ready, 1)
                        else:
                            bank = filled(at, f"score{b}")
                            cols = slice(NB + KJ * b, NB + KJ * (b + 1))
                            link(at, dve.reduce_max(rtotal[0:KR, cols],
                                                    bank[0:KR, 0:KJ * S].rearrange("p (j s) -> p j s", j=KJ), AX.X))
                            dve.tensor_scalar(negmax[0:KR, cols], rtotal[0:KR, cols], -FRONT_SCALE, None, ALU.mult)\
                                .then_inc(negmax_ready, 1)
                    for b in range(NB):
                        k = NB * n + b
                        if n != 1:
                            dve.wait_ge(exp_ready, at.at("exp", k + 1))
                            link(at, dve.reciprocal(rtotal[0:S, b:b + 1], total[0:S, b:b + 1]))
                            dve.tensor_scalar(prob[0:S, b, 0:S2], prob[0:S, b, 0:S2], rtotal[0:S, b:b + 1], None, ALU.mult)\
                                .then_inc(prob_ready, 1)
                        else:
                            cols = slice(NB + KJ * b, NB + KJ * (b + 1))
                            dve.wait_ge(exp_ready, at.at("exp", k + 1))
                            link(at, dve.reciprocal(rtotal[0:KR, cols], total[0:KR, cols]))
                            dve.tensor_tensor(probT[:, b, :, 0:S], prob[:, b, 0:KJ * S].rearrange("p (j s) -> p j s", j=KJ),
                                              rtotal[0:KR, cols].unsqueeze(2).broadcast_to([KR, KJ, S]), ALU.mult)\
                                .then_inc(prob_ready, 1)
                    if n != 1:
                        bank = filled(at, "tr1")
                        dve.tensor_copy(probT[:, 1, :, 0:S], bank[0:KR, 0:KJ * S].rearrange("p (j s) -> p j s", j=KJ))\
                            .then_inc(taken["tr1"], 1)
                    bank = filled(at, "sum1")
                    dve.tensor_copy(fcT[:, S:T2], bank[:, 0:S]).then_inc(taken["sum1"], 1)
                    if n != 1:
                        bank = filled(at, "proj1")
                        plus(faT[:, 1, :], bank[:, 0:T2], fcol[:, n, 2, 1:2]).then_inc(taken["proj1"], 1)
                        dve.wait_ge(resid_ready, at.at("resid", at.next("resid") + 1))
                    bank = filled(at, "proj1")
                    dve.tensor_tensor(tw[:, :, :], bank[0:S, 0:NB * E].rearrange("p (b e) -> p b e", b=NB), tw[:, :, :],
                                      ALU.add).then_inc(taken["proj1"], 1)
                    if n == 1:
                        dve.wait_ge(taken["proj1"], at.emptied("proj1", at.n["proj1"]))
                        statistics(at, tw)
                        wait_rstd(at)
                        for b in range(NB):
                            ins = normalise(tn[:, b, :], tw, b)
                        link(at, ins)
                        link(at, dve.tensor_tensor(tn[:, :, :], tn[:, :, :],
                                                   fbias[0:S, 3, :].unsqueeze(1).broadcast_to([S, NB, E]), ALU.mult))
                        dve.tensor_tensor(tw[:, :, :], tn[:, :, :],
                                          fbias[0:S, 4, :].unsqueeze(1).broadcast_to([S, NB, E]), ALU.add)\
                            .then_inc(tn_ready, 1)
                dve.wait_ge(taken["proj1"], at.emptied("proj1", at.n["proj1"]))
                dve.tensor_copy(t_all[:, ds(p * NB, NB), :], tw[:, :, :])
                pair_ctx = ctxT[:, ds(p * (NB * S2), NB * S2)]
                dve.scalar_tensor_tensor(pair_ctx, cmask[:, :, :].rearrange("p b s -> p (b s)"), 0.0, pair_ctx,
                                         ALU.not_equal, ALU.mult).then_inc(front_done, 1)

            dve.wait_ge(front_done, PAIRS)

            def normed(at, a):
                wait_rstd(at)
                for b in range(NB):
                    normalise(tn[:, b, :], a, b).then_inc(tn_ready, 1)

            def diagonal(at, name, o, c):
                bank = filled(at, name)
                for h in range(2):
                    ins = dve.tensor_copy(o[h * D:(h + 1) * D, c, h, :], bank[h * D:(h + 1) * D, 0:T2])
                ins.then_inc(taken[name], 1)

            def chunk(at, o, n):
                bank = filled(at, "proj1")
                dve.tensor_copy(o, bank[0:o.shape[0], 0:n]).then_inc(taken["proj1"], 1)

            def values(at, b):
                chunk(at, v[:, b, 512:1024], 512)

            def new_smask(it):
                dve.wait_ge(smask_loaded, (it + 1) * 16)
                dve.tensor_scalar(smask0[:, :, :], smask[:, :, :], 0.0, None, ALU.is_equal).then_inc(smask_used, 1)
                gate(smask_used, it + 1)

            def self_reciprocals(at, t):
                cols = slice(G * t, G * t + G)
                dve.wait_ge(exp_ready, at.at("exp", t + 1))
                dve.reciprocal(rtotal[0:S, cols], total[0:S, cols]).then_inc(rtotal_ready, 1)

            def queries(at, chunks):
                for c in chunks:
                    chunk(at, qT[:, c, :], T2)

            def self_maxima(at, t, here, meanwhile=None):
                name = f"score{t % 2}"
                b, cols = t // GB, slice(G * t, G * t + G)
                gate(ready[name], at.at(name, t // 2 + 1))
                four = banks[name][0:S, 0:G * S].rearrange("p (h k) -> p h k", h=G)
                dve.copy_predicated(four, smask0[:, b, :].unsqueeze(1).broadcast_to([S, G, S]),
                                    masked[:, 0:1].unsqueeze(1).broadcast_to([S, G, S])).then_inc(dve_step, 1)
                if meanwhile:
                    meanwhile()
                linked(here)
                dve.reduce_max(rtotal[0:S, cols], four, AX.X).then_inc(dve_step, 1)
                if t > 0:
                    self_reciprocals(at, t - 1)
                linked(here)
                dve.tensor_scalar(negmax[0:S, cols], rtotal[0:S, cols], -SCALE, None, ALU.mult).then_inc(negmax_ready, 1)

            at = Place(START)
            new_smask(0)
            first = t_all[:, 0:NB, :]
            statistics(at, first)
            normed(at, first)
            for b in range(NB):
                values(at, b)
            queries(at, range(1, HC, 2))
            for c in range(1, HC, 2):
                diagonal(at, "proj1", k_diag, c)
            for t in range(EARLY):
                self_maxima(Place(MAIN_LOOP), t, at)
            at.check()
            with dve.Fori(0, L) as l:
                with dve.Fori(0, PAIRS) as p:
                    it = l * PAIRS + p
                    at = Place(MAIN_LOOP, it)
                    next_tokens = t_all[:, ds((p + 1) % PAIRS * NB, NB), :]

                    def residual(o, with_statistics=True, between=None):
                        dve.wait_ge(resid_ready, at.at("resid", at.next("resid") + 1))
                        for b, name in enumerate(("sum1", "proj1")):
                            if between and b == 1:
                                between()
                            bank = filled(at, name)
                            dve.tensor_tensor(o[:, b, :], bank[0:S, 0:E], tw[:, b, :], ALU.add).then_inc(taken[name], 1)
                            if with_statistics:
                                dve.wait_ge(taken[name], at.emptied(name, at.n[name]))
                                ins = dve.bn_stats(stats[:, b, :], o[:, b, :])
                        if with_statistics:
                            variances(at, ins)

                    for t in range(EARLY, SG + SA_LAG + SUM_LAG):
                        def empty_sum1():
                            g = t - SA_LAG - SUM_LAG
                            if 0 <= g < SG and g % 2 == 1:
                                b, c = g // GB, g % GB * 2
                                bank = filled(at, "sum1")
                                for h in range(2):
                                    r = slice(h * D, (h + 1) * D)
                                    ins = dve.tensor_copy(oT[r, c:c + 2, b * S:(b + 1) * S],
                                                          bank[r, 0:2 * T2].rearrange("p (n h s) -> p n h s", n=2, h=2)[:, :, h, :])
                                ins.then_inc(taken["sum1"], 1)

                        if t < SG:
                            self_maxima(at, t, at, meanwhile=empty_sum1)
                        else:
                            empty_sum1()
                        if 0 <= t - SA_LAG < SG and (t - SA_LAG) % 2 == 1:
                            bank = filled(at, "tr1")
                            dve.tensor_copy(probT[0:S, 1, 0, :], bank[0:S, 0:G * S]).then_inc(taken["tr1"], 1)
                        if t == SG:
                            self_reciprocals(at, SG - 1)
                            statistics(at, next_tokens)
                        if t == SG + 2:
                            normed(at, next_tokens)
                    dve.wait_ge(cmask_loaded, (it + 1) * 16)
                    dve.tensor_scalar(cbias[:, :, :], cmask[0:S, :, :], 0.0, MASKED, ALU.is_equal, ALU.mult)\
                        .then_inc(cmask_used, 1)
                    gate(cmask_used, it + 1)
                    residual(tw)
                    values(at, 0)
                    normed(at, tw)
                    values(at, 1)
                    for n in range(1, HC + 2, 2):
                        if n < HC:
                            diagonal(at, "sum1", q_diag, n)
                        if n >= 2:
                            chunk(at, qcT[:, 2 * n - 4:2 * n - 2, :].rearrange("p h t -> p (h t)"), 2 * T2)
                    for t in range(NH + CA_LAG + SUM_LAG):
                        if t < NH:
                            name = f"score{t % 2}"
                            col = G * SG + t
                            if t >= RAWS:
                                gate(exp_ready, at.at("exp", SG + t - RAWS + 1))
                            gate(ready[name], at.at(name, (SG + t) // 2 + 1))
                            dve.tensor_tensor_reduce(out=raw[:, t % RAWS, :], in0=banks[name][0:S, 0:S2],
                                                     in1=cbias[:, t // H, :], scale=-SCALE, scalar=3.4e38,
                                                     op0=ALU.add, op1=ALU.min, accum_out=negmax[0:S, col:col + 1])\
                                .then_inc(negmax_ready, 1)
                        if 0 <= t - 1 < NH:
                            col = G * SG + t - 1
                            dve.wait_ge(exp_ready, at.at("exp", SG + t))
                            dve.reciprocal(rtotal[0:S, col:col + 1], total[0:S, col:col + 1]).then_inc(rtotal_ready, 1)
                        if 0 <= t - CA_LAG < NH and (t - CA_LAG) % 2 == 1:
                            i = t - CA_LAG
                            if i % G == 1:
                                g = SUM_CA + i // G
                                dve.wait_ge(ready[f"sum{g % 2}"], at.at(f"sum{g % 2}", g // 2))
                            bank = filled(at, "tr1")
                            dve.tensor_copy(probT[:, i // G % 2, :, i % G * S:(i % G + 1) * S],
                                            bank[0:KR, 0:KJ * S].rearrange("p (j s) -> p j s", j=KJ)).then_inc(taken["tr1"], 1)
                        if 0 <= t - CA_LAG - SUM_LAG < NH and (t - CA_LAG - SUM_LAG) % (2 * G) == 2 * G - 1:
                            g = (t - CA_LAG - SUM_LAG) // G
                            b, h = g // GB, g % GB * G
                            bank = filled(at, "sum1")
                            dve.tensor_copy(cT[:, h:h + G, b * S:(b + 1) * S],
                                            bank[:, 0:G * S].rearrange("p (h s) -> p h s", h=G)).then_inc(taken["sum1"], 1)
                        if KEY_STEPS.get(t, 0) % 2 == 1:
                            diagonal(at, "proj1", k_diag, KEY_STEPS[t])
                    for c in range(1, HC, 2):
                        chunk(at, oT[:, c, :], T2)
                    residual(tw)
                    queries(at, (1,))
                    normed(at, tw)
                    queries(at, range(3, HC, 2))
                    new_smask(it + 1)
                    early = Place(MAIN_LOOP, it + 1)
                    for c in range(1, FC, 2):
                        bank = filled(at, "proj1")
                        dve.tensor_scalar(hT[:, c, :], bank[:, 0:T2], f_b1[:, c:c + 1], 0.0, ALU.add, ALU.max)\
                            .then_inc(taken["proj1"], 1)
                    for t in range(EARLY - 1):
                        self_maxima(early, t, at)
                    residual(t_all[:, ds(p * NB, NB), :], False, between=lambda: self_maxima(early, EARLY - 1, at))
                    assert all(at.n[k] == MAIN[k] for k in ("proj1", "tr1", "sum1", "dve", "stats", "resid"))


_DECODER = ["sa_kv", "sa_q", "sa_ow", "sa_ob", "ca_kv", "ca_q", "ca_ow", "ca_ob", "ff_w1", "ff_b1", "ff_w2", "ff_b2",
            "pre_g", "pre_b", "norm_g", "norm_b"]
_COLUMNS = ("bq", "bk", "bv", "ff_b1", "pre_g", "pre_b", "norm_g", "norm_b")
_FRONT = [["Wq", "bq", "Wk", "bk", "Wv", "bv", "Wo", "bo"], ["Wq", "bq", "Wk", "bk", "Wv", "bv", "gamma", "beta"],
          ["Wq", "bq", "Wk", "bk", "Wv", "bv", "Wo", "bo"]]


def kernel(**inputs):
    import numpy as _np
    import concourse.bacc as _bacc
    from concourse import mybir as _mybir
    from concourse.bass_utils import run_bass_kernel_spmd as _run

    nc = _bacc.Bacc("TRN2", target_bir_lowering=False, num_devices=1)
    arrays = {}

    def give(name, a):
        a = _np.ascontiguousarray(a)
        arrays[name] = a
        return nc.dram_tensor(name, a.shape, _mybir.dt.from_np(a.dtype), kind="ExternalInput").ap()

    x = _np.asarray(inputs["x"])
    ctx = _np.asarray(inputs["ctx_512"])
    mask = _np.asarray(inputs["mask_Bx1xS2_if1"])
    hd = inputs["L3_xattn_sa_q"].shape[2]

    def columns(a):
        a = _np.asarray(a)
        return _np.swapaxes(a.reshape(a.shape[:-1] + (-1, 128)), -1, -2)

    dec = {n: give(n, (columns if n in _COLUMNS else _np.asarray)(inputs["L3_xattn_" + n])) for n in _DECODER}
    dec["ca_kT"] = give("ca_kT", _np.asarray(inputs["L3_xattn_ca_kv"])[:, :, 0:hd].transpose(0, 2, 1))
    front = [{n: give(f"L{i}_{n}", (columns if n in _COLUMNS else _np.asarray)(inputs[f"L{i}_xattn_{n}"])) for n in names}
             for i, names in enumerate(_FRONT)]
    front[1]["bv_row"] = give("L1_bv_row", _np.asarray(inputs["L1_xattn_bv"]))
    args = [give("x", x), give("ctx", ctx), give("ctx_T", ctx.reshape(-1, ctx.shape[2]).T),
            give("self_mask", _np.asarray(inputs["mask_BxSxS_ik0"])), give("ctx_mask", mask.reshape(mask.shape[0], -1))]
    out = nc.dram_tensor("out", x.shape, _mybir.dt.float32, kind="ExternalOutput").ap()
    attention_layers(nc, *args, front, dec, out)
    return _run(nc, [arrays], core_ids=[0]).results[0]["out"]
```

```python
import concourse.bass as bass
from concourse import mybir
from contextlib import ExitStack


def attention_layers(nc, x, ctx_nat, ctx_tr, self_mask, ctx_mask, front, dec, out):
    f32, f32r, i32 = mybir.dt.float32, mybir.dt.float32r, mybir.dt.int32
    ALU, ACT, AX = mybir.AluOpType, mybir.ActivationFunctionType, mybir.AxisListType
    ds = bass.ds

    B, S, E = x.shape
    _, S2, C = ctx_nat.shape
    L, _, HDIM = dec["sa_q"].shape
    P = 128
    EK = E // P
    D = 64
    H = HDIM // D
    HC = HDIM // P
    FC = dec["ff_w1"].shape[2] // P
    NB = 2
    PAIRS = B // NB
    T2 = NB * S
    KJ = 3
    KR = S2 // KJ
    G = 4
    GB = H // G
    SG = NB * GB
    NH = NB * H
    V2 = HDIM // 512
    S2E = S2 + S2 % 2
    FRONT_SCALE = float(E) ** -0.5
    SCALE = float(D) ** -0.5
    MASKED = -1.0e9 / SCALE

    NU = 2
    ROUNDS = PAIRS // NU
    assert B == ROUNDS * NU * NB
    FRONT = {"proj0": 14 * NU, "proj1": 14 * NU, "score0": 3 * NU, "score1": 3 * NU, "tr0": 2 * NU, "tr1": 2 * NU,
             "sum0": 3 * NU, "sum1": 3 * NU, "stats": NU, "tn": NU, "resid": 2 * NU, "negmax": 3 * NB * NU,
             "exp": 3 * NB * NU, "prob": 3 * NB * NU, "rtotal": 0, "dve": (4 * NB + 3) * NU, "pool": NU, "high": 0}
    SA_OUT = 0
    CA_OUT = 1 + V2 + 3 * HC // 2
    Q_END = CA_OUT + 1 + HC // 2
    FF_OUT = Q_END + FC // 2
    SA_LAG, CA_LAG = 3, 4
    SUM_LAG = 2
    PROBS = 6
    KEY_STEPS = {(1 if c < HC // 2 else NH - HC // 2 + 1) + c: c for c in range(HC)}
    EARLY = SA_LAG + 1
    KT = 1 + V2
    SUM_Q = SG + 2
    SUM_CA = SUM_Q + HC
    MAIN = {"proj0": FF_OUT - 1, "proj1": FF_OUT + 1, "score0": (SG + NH) // 2, "score1": (SG + NH) // 2,
            "tr0": (SG + NH) // 2, "tr1": (SG + NH) // 2, "sum0": SG + HC // 2 + 2, "sum1": SG + HC // 2 + 3,
            "stats": 3, "tn": 3 * NB, "resid": 3, "negmax": SG + NH, "exp": SG + NH,
            "prob": SG + NH, "rtotal": SG + NH, "dve": 3 + 2 * SG, "pool": 4, "high": HC}
    BETWEEN = {"proj0": 1 + V2 + HC, "proj1": V2 + HC, "stats": 1, "tn": NB, "dve": 1 + 2 * EARLY, "pool": 1}
    FRONT_LOOP, START, MAIN_LOOP = range(3)

    class Place:

        def __init__(self, part, it=0):
            self.part, self.it, self.n = part, it, {}

        def base(self, name):
            if self.part == FRONT_LOOP:
                return self.it * FRONT[name]
            if self.part == START:
                return ROUNDS * FRONT[name]
            return ROUNDS * FRONT[name] + BETWEEN.get(name, 0) + self.it * MAIN[name]

        def at(self, name, k):
            return self.base(name) + k

        def emptied(self, name, k):
            return self.base(name) + k + 1

        def next(self, name):
            self.n[name] = self.n.get(name, 0) + 1
            return self.n[name] - 1

        def check(self):
            want = (FRONT, BETWEEN, MAIN)[self.part]
            for name, n in self.n.items():
                assert n == want[name], (name, n, want[name])

    scope = ExitStack()
    with scope:
        def sb(name, shape, dt=f32):
            return scope.enter_context(nc.sbuf_tensor(name, shape, dt))

        def in_one_place(name, name_r, shape, dt=f32, dt_r=f32r):
            with nc.sbuf_tensor(name, shape, dt) as first:
                pass
            return first, sb(name_r, shape, dt_r)

        def sem(name):
            return scope.enter_context(nc.semaphore(name))

        ident = sb("ident", [P, P])
        eps = sb("eps", [S, 2, NB])
        minus_half = sb("minus_half", [S, NB])
        masked = sb("masked", [S, 1])
        t_all = sb("t_all", [S, B, E])
        ctxT = sb("ctxT", [P, B * S2])
        ctxN = sb("ctxN", [KR, NB, KJ, C])
        ctx_parts = sb("ctx_parts", [P, 2, NB, S2E], f32r)
        w_q = sb("w_q", [P, EK, HDIM])
        w_kv = sb("w_kv", [P, EK, 2 * HDIM])
        w_o = sb("w_o", [P, HC, E])
        c_q = sb("c_q", [P, EK, HDIM])
        c_kT = sb("c_kT", [P, HC, C])
        c_v = sb("c_v", [P, HDIM])
        c_o = sb("c_o", [P, HC, E])
        f_1 = sb("f_1", [P, EK, FC * P])
        f_2 = sb("f_2", [P, FC, E])
        f_b1 = sb("f_b1", [P, FC])
        norm = sb("norm", [P, 2, EK])
        pre = sb("pre", [P, 2, EK])
        o_bias = sb("o_bias", [S, 3, E])
        tw = sb("tw", [S, NB, E])
        stats = sb("stats", [S, NB, 6])
        mv2 = sb("mv", [S, NU, NB, 2])
        mv = mv2[:, 0]
        veps = sb("veps", [S, NU, NB])
        rstd2 = sb("rstd", [S, NU, NB])
        rstd = rstd2[:, 0]
        tnT = sb("tnT", [P, EK, T2])
        tnT_next = sb("tnT_next", [P, EK, T2])
        k_diag = sb("k_diag", [P, HC, 2, T2])
        q_diag = k_diag
        v_all = sb("v", [P, NB * HDIM])
        v = v_all[0:S, :].rearrange("p (b n) -> p b n", b=NB)
        oT = sb("oT", [P, HC, T2])
        qT = oT
        qcT, qc_high = in_one_place("qcT", "qc_high", [P, H, T2])
        before_low, qc_low = in_one_place("before_low", "qc_low", [P, H, T2])
        tn = qcT[0:S, :, :].rearrange("p h t -> p (h t)")[:, 0:NB * E].rearrange("p (b e) -> p b e", b=NB)
        cT = qcT
        hT = qcT[:, 0:FC, :]
        prob = sb("prob", [KR, PROBS, G * S])
        probT = sb("probT", [KR, 2, KJ, G * S])
        negmax = sb("negmax", [P, G * SG + NH])
        total = sb("total", [P, G * SG + NH])
        rtotal = sb("rtotal", [P, G * SG + NH])
        smask = sb("smask", [S, NB, S], i32)
        smask0 = sb("smask0", [S, NB, S], i32)
        cmask, cbias = in_one_place("cmask", "cbias", [S, NB, S2], i32, f32)
        FW = 2 * EK * E + 2 * E
        q_flat = qcT[:, :, :].rearrange("p h t -> p (h t)")
        fw = [q_flat[:, 0:FW], q_flat[:, FW:2 * FW], oT[:, :, :].rearrange("p c t -> p (c t)")[:, 0:FW]]
        fwq = [a[:, 0:EK * E].rearrange("p (k n) -> p k n", k=EK) for a in fw]
        fwo = [a[:, EK * E:2 * EK * E].rearrange("p (k n) -> p k n", k=EK) for a in fw]
        fwk = [a[:, 2 * EK * E:2 * EK * E + E] for a in fw]
        fwv = [a[:, 2 * EK * E + E:FW] for a in fw]
        one = f_1[:, :, :].rearrange("p k n -> p (k n)")
        two = f_2[:, :, :].rearrange("p k n -> p (k n)")
        k_end, q_end = NB * EK * S2, NB * EK * S2 + EK * T2
        fkT = [a[:, 0:k_end].rearrange("p (b k n) -> p b k n", b=NB, k=EK) for a in (v_all, two)]
        fqT = [a.rearrange("p (k n) -> p k n", k=EK) for a in (v_all[:, k_end:q_end], one[:, 0:EK * T2])]
        ftnT = [tnT, one[:, EK * T2:2 * EK * T2].rearrange("p (k n) -> p k n", k=EK)]
        faT = [tnT_next, one[:, 2 * EK * T2:3 * EK * T2].rearrange("p (k n) -> p k n", k=EK)]
        fcT = [one[:, (3 * EK + u) * T2:(3 * EK + u + 1) * T2] for u in range(NU)]
        ftw = [tw, two[0:S, k_end:k_end + NB * E].rearrange("p (b e) -> p b e", b=NB)]
        ftn = [a[0:S, 0:NB * E].rearrange("p (b e) -> p b e", b=NB) for a in (v_all, two)]
        three = c_o[:, :, :].rearrange("p k n -> p (k n)")
        fctxN = [ctxN[:, :, :, :], three[0:KR, 0:NB * KJ * C].rearrange("p (b j c) -> p b j c", b=NB, j=KJ)]
        four = c_q[:, :, :].rearrange("p k n -> p (k n)")
        fcmask = [four[:, u * NB * S2:(u + 1) * NB * S2].bitcast(i32).rearrange("p (b s) -> p b s", b=NB) for u in range(NU)]
        fcol = sb("fcol", [P, 3, 3, EK])
        fbias = before_low[0:KR].rearrange("p h t -> p (h t)")[:, 0:5 * E].rearrange("p (a n) -> p a n", a=5)

        banks = {n: scope.enter_context(nc.psum_tensor(n, [P, 512], f32))
                 for n in ("proj0", "proj1", "score0", "score1", "tr0", "tr1", "sum0", "sum1")}
        ready = {n: sem(f"{n}_ready") for n in banks}
        taken = {n: sem(f"{n}_taken") for n in banks if "score" not in n}

        setup_ids = sem("setup_ids")
        setup_done = sem("setup_done")
        front_loaded = [sem(f"front_loaded{n}") for n in range(3)]
        rows_loaded = sem("rows_loaded")
        x_loaded = sem("x_loaded")
        ctx_loaded = sem("ctx_loaded")
        smask_loaded = sem("smask_loaded")
        cmask_loaded = sem("cmask_loaded")
        smask_used = sem("smask_used")
        cbias_written = sem("cbias_written")
        front_done = sem("front_done")
        loaded = {n: sem(f"{n}_loaded") for n in
                  ("w_q", "w_kv", "w_o", "c_q", "c_kT", "c_v", "c_o", "f_1", "f_2", "small")}
        dve_step = sem("dve_step")
        pool_step = sem("pool_step")
        passed = sem("passed")
        stats_ready = sem("stats_ready")
        rstd_ready = sem("rstd_ready")
        tn_ready = sem("tn_ready")
        resid_ready = sem("resid_ready")
        negmax_ready = sem("negmax_ready")
        exp_ready = sem("exp_ready")
        rtotal_ready = sem("rtotal_ready")
        prob_ready = sem("prob_ready")
        pool_passed = sem("pool_passed")
        split_ready = sem("split_ready")
        high_ready = sem("high_ready")
        stored = sem("stored")

        SMALL = 6
        FRONT_DMAS = (8, 6, 7)
        ROW_DMAS = 7

        block = scope.enter_context(nc.Block())

        @block.sync
        def _(sp):
            def load_pair_x(p, u):
                sp.dma_start(ftw[u][:, :, :], x[ds(p * NB, NB)].rearrange("b s e -> s b e")).then_inc(x_loaded, 16)
                sp.dma_start(fcmask[u], ctx_mask[ds(p * NB, NB)].partition_broadcast(P)).then_inc(x_loaded, 16)

            def load_pair_ctx(p, u=0):
                sp.dma_start(fctxN[u], ctx_nat[ds(p * NB, NB)].rearrange("b (j r) c -> r b j c", r=KR))\
                    .then_inc(ctx_loaded, 16)

            def load_pair_smask(p):
                sp.dma_start(smask[:, :, :], self_mask[ds(p * NB, NB)].rearrange("b q k -> q b k")).then_inc(smask_loaded, 16)

            def load_pair_cmask(p):
                sp.dma_start(cmask[:, :, :], ctx_mask[ds(p * NB, NB)].partition_broadcast(S)).then_inc(cmask_loaded, 16)

            def chunks(a, l):
                return a[ds(l, 1)].rearrange("o (k p) n -> p (o k) n", p=P)

            def load_qkv(l):
                sp.dma_start(w_q[:, :, :], chunks(dec["sa_q"], l)).then_inc(loaded["w_q"], 16)
                sp.dma_start(w_kv[:, :, :], chunks(dec["sa_kv"], l)).then_inc(loaded["w_kv"], 16)

            def load_w_o(l):
                sp.dma_start(w_o[:, :, :], chunks(dec["sa_ow"], l)).then_inc(loaded["w_o"], 16)

            def load_ca(l):
                sp.dma_start(c_kT[:, :, :], chunks(dec["ca_kT"], l)).then_inc(loaded["c_kT"], 16)
                sp.dma_start(c_v[:, :], dec["ca_kv"][ds(l, 1), :, HDIM:2 * HDIM].rearrange("o c n -> c (o n)"))\
                    .then_inc(loaded["c_v"], 16)

            def load_c_q_o(l):
                sp.dma_start(c_q[:, :, :], chunks(dec["ca_q"], l)).then_inc(loaded["c_q"], 16)
                sp.dma_start(c_o[:, :, :], chunks(dec["ca_ow"], l)).then_inc(loaded["c_o"], 16)

            def load_ff(l):
                sp.dma_start(f_1[:, :, :], chunks(dec["ff_w1"], l)).then_inc(loaded["f_1"], 16)
                sp.dma_start(f_2[:, :, :], chunks(dec["ff_w2"], l)).then_inc(loaded["f_2"], 16)

            def load_small(l):
                sp.dma_start(f_b1[:, :], dec["ff_b1"][ds(l, 1)].rearrange("o p k -> p (o k)")).then_inc(loaded["small"], 16)
                for n, name in enumerate(("pre_g", "pre_b")):
                    sp.dma_start(pre[:, n, :], dec[name][ds(l, 1)].rearrange("o p k -> p (o k)"))\
                        .then_inc(loaded["small"], 16)
                for n, name in enumerate(("sa_ob", "ca_ob", "ff_b2")):
                    sp.dma_start(o_bias[:, n, :], dec[name][ds(l, 1)].partition_broadcast(S)).then_inc(loaded["small"], 16)

            def load_rows(indices, rows):
                for n, a in zip(indices, rows):
                    sp.dma_start(fbias[:, n, :], a.partition_broadcast(KR)).then_inc(rows_loaded, 16)

            for u in range(NU):
                load_pair_x(u, u)
            for n in range(3):
                here = front_loaded[n]
                sp.dma_start(fwq[n], front[n]["Wq"].rearrange("(k p) n -> p k n", p=P)).then_inc(here, 16)
                sp.dma_start(fwk[n], front[n]["Wk"]).then_inc(here, 16)
                if n == 0:
                    sp.dma_start(ctxT[:, :], ctx_tr).then_inc(here, 16)
                for j, name in enumerate(("bq", "bk", "bv")):
                    sp.dma_start(fcol[:, n, j, :], front[n][name]).then_inc(here, 16)
                sp.dma_start(fwv[n], front[n]["Wv"]).then_inc(here, 16)
                if n != 1:
                    sp.dma_start(fwo[n], front[n]["Wo"].rearrange("(k p) n -> p k n", p=P)).then_inc(here, 16)
                if n == 0:
                    for u in range(NU):
                        load_pair_ctx(u, u)
                    load_rows(range(5), (front[0]["bo"], front[2]["bo"], front[1]["bv_row"], front[1]["gamma"],
                                         front[1]["beta"]))
            for n, name in enumerate(("norm_g", "norm_b")):
                sp.dma_start(norm[:, n, :], dec[name]).then_inc(rows_loaded, 16)
            load_qkv(0)
            load_w_o(0)
            load_ca(0)
            load_small(0)
            with sp.Fori(1, ROUNDS) as i:
                for u in range(NU):
                    sp.wait_ge(front_done, (i - 1) * NU + u + 1)
                    load_pair_x(i * NU + u, u)
                    load_pair_ctx(i * NU + u, u)
            sp.wait_ge(front_done, PAIRS)
            load_pair_ctx(0)
            load_pair_smask(0)
            load_pair_cmask(0)
            load_c_q_o(0)
            load_ff(0)

            def next_pair(at, p):
                sp.wait_ge(smask_used, at.it + 1)
                load_pair_smask(p)
                sp.wait_ge(ready["proj1"], at.at("proj1", CA_OUT + 1))
                load_pair_cmask(p)
                load_pair_ctx(p)

            def layer(l, last):
                with sp.Fori(1, PAIRS) as p:
                    next_pair(Place(MAIN_LOOP, l * PAIRS + p - 1), p)
                at = Place(MAIN_LOOP, l * PAIRS + PAIRS - 2)
                sp.wait_ge(ready["proj1"], at.at("proj1", Q_END))
                if last:
                    sp.wait_ge(smask_used, L * PAIRS)
                    load_pair_smask(0)
                    sp.sem_inc(loaded["w_q"], 16)
                    sp.sem_inc(loaded["w_kv"], 16)
                    return
                load_qkv(l + 1)
                at = Place(MAIN_LOOP, l * PAIRS + PAIRS - 1)
                sp.wait_ge(ready["proj1"], at.at("proj1", SA_OUT + 1))
                load_w_o(l + 1)
                next_pair(at, 0)
                load_ca(l + 1)
                load_c_q_o(l + 1)
                sp.wait_ge(taken["proj1"], at.emptied("proj1", FF_OUT + 1))
                load_small(l + 1)
                load_ff(l + 1)

            with sp.Fori(0, L - 1) as l:
                layer(l, False)
            layer(L - 1, True)
            sp.wait_ge(taken["proj1"], Place(MAIN_LOOP, L * PAIRS).emptied("proj1", 0))
            sp.dma_start(out.rearrange("b s e -> s b e"), t_all[:, :, :]).then_inc(stored, 16)
            sp.wait_ge(stored, 16)

        @block.gpsimd
        def _(pool):
            pool.memset(ident[:, :], 0.0).then_inc(setup_ids, 1)
            pool.memset(eps[:, 0, :], 1e-5)
            pool.memset(eps[:, 1, :], 1e-6)
            pool.memset(minus_half[:, :], -0.5)
            pool.memset(masked[:, :], MASKED)
            pool.memset(cbias[:, :, :], 0.0)
            pool.memset(k_diag[:, :, :, :], 0.0).then_inc(setup_ids, 1)
            pool.wait_ge(setup_ids, 2)
            pool.tensor_copy(ctx_parts[:, :, :, S2:S2E], k_diag[:, 0, 0, 0:2 * NB * (S2E - S2)]
                             .rearrange("p (n b s) -> p n b s", n=2, b=NB))
            pool.affine_select(out=ident[:, :], in_=ident[:, :], compare_op=ALU.not_equal, fill=1.0, base=0,
                               pattern=[[-1, P]], channel_multiplier=1).then_inc(setup_done, 1)
            for name in taken:
                pool.sem_inc(taken[name], 1)

            def inverse_std(at, which, u=0):
                k = at.next("stats")
                pool.wait_ge(stats_ready, at.at("stats", k + 1))
                pool.tensor_tensor(veps[:, u], mv2[:, u, :, 1], eps[:, which, :], ALU.add).then_inc(pool_step, 1)
                pool.wait_ge(pool_step, at.at("pool", at.next("pool") + 1))
                pool.tensor_tensor(rstd2[:, u], veps[:, u], minus_half[:, :], ALU.pow).then_inc(rstd_ready, 1)

            def add_bias(bias, tw=tw):
                pool.tensor_tensor(tw[:, :, :], tw[:, :, :], bias.unsqueeze(1).broadcast_to([S, NB, E]), ALU.add)\
                    .then_inc(resid_ready, 1)

            pool.wait_ge(rows_loaded, 16 * ROW_DMAS)
            with pool.Fori(0, ROUNDS) as i:
                at = Place(FRONT_LOOP, i)
                for u in range(NU):
                    pool.wait_ge(ready["proj0"], at.at("proj0", u + 1))
                    add_bias(fbias[0:S, 0, :], ftw[u])
                for u in range(NU):
                    inverse_std(at, 1, u)
                for u in range(NU):
                    pool.wait_ge(ready["proj0"], at.at("proj0", 9 * NU + u + 1))
                    add_bias(fbias[0:S, 1, :], ftw[u])

            def normalise_group(at, g):
                pr = prob[0:S, g % PROBS, :].rearrange("p (h k) -> p h k", h=G)
                pool.wait_ge(rtotal_ready, at.at("rtotal", g + 1))
                pool.tensor_tensor(pr, pr, rtotal[0:S, G * g:G * g + G].unsqueeze(2).broadcast_to([S, G, S]), ALU.mult)\
                    .then_inc(prob_ready, 1)

            inverse_std(Place(START), 0)
            for g in range(EARLY - 1):
                normalise_group(Place(MAIN_LOOP), g)
            with pool.Fori(0, L) as l:
                with pool.Fori(0, PAIRS) as p:
                    at = Place(MAIN_LOOP, l * PAIRS + p)
                    pool.wait_ge(loaded["small"], (l + 1) * (16 * SMALL))
                    pool.wait_ge(taken["proj1"], at.emptied("proj1", 0))
                    pool.tensor_tensor(tw[:, :, :], t_all[:, ds(p * NB, NB), :],
                                       o_bias[:, 0, :].unsqueeze(1).broadcast_to([S, NB, E]), ALU.add).then_inc(resid_ready, 1)
                    for g in range(EARLY - 1, SG):
                        normalise_group(at, g)
                    inverse_std(at, 0)
                    whole = ctxT[:, ds(p * (NB * S2), NB * S2)].rearrange("p (b s) -> p b s", b=NB)
                    pool.tensor_copy(ctx_parts[:, 0, :, 0:S2], whole).then_inc(pool_step, 1)
                    pool.wait_ge(pool_step, at.at("pool", at.next("pool") + 1))
                    pool.sem_inc(pool_passed, 1)
                    pool.tensor_tensor(ctx_parts[:, 1, :, 0:S2], whole, ctx_parts[:, 0, :, 0:S2].bitcast(f32), ALU.subtract)\
                        .then_inc(split_ready, 1)
                    for n in (1, 2):
                        inverse_std(at, 0)
                        pool.wait_ge(tn_ready, at.at("tn", NB * (n + 1)))
                        add_bias(o_bias[:, n, :])
                        if n == 1:
                            for i in range(NH):
                                row = prob[0:S, i % PROBS, 0:S2]
                                pool.wait_ge(rtotal_ready, at.at("rtotal", SG + i + 1))
                                pool.tensor_tensor(row, row, rtotal[0:S, G * SG + i:G * SG + i + 1].broadcast_to([S, S2]),
                                                   ALU.mult).then_inc(prob_ready, 1)
                    for g in range(EARLY - 1):
                        normalise_group(Place(MAIN_LOOP, l * PAIRS + p + 1), g)
                    at.check()

        @block.tensor
        def _(pe):
            def fill(at, name):
                if name in taken:
                    pe.wait_ge(taken[name], at.emptied(name, at.next(name)))
                return banks[name]

            def done(ins, name):
                ins.then_inc(ready[name], 1)

            def transposes_of(at, a, name="proj0"):
                bank = fill(at, name)
                for k in range(EK):
                    for b in range(NB):
                        ins = pe.transpose(bank[:, k * T2 + b * S:k * T2 + (b + 1) * S], a[:, b, k * P:(k + 1) * P],
                                           ident[0:S, 0:S])
                done(ins, name)

            def project(at, name, weights, moving):
                bank = fill(at, name)
                for k, (w, m) in enumerate(zip(weights, moving)):
                    ins = pe.matmul(bank[0:w.shape[1], 0:m.shape[1]], w, m, start=k == 0, stop=k == len(weights) - 1)
                done(ins, name)

            def out_rows(at, stationary, weights, written=False, slots=("proj1",), between=None):
                counts = dict(at.n)
                for b in range(NB):
                    if between and b == 1:
                        between()
                    if b < len(slots):
                        bank, col = fill(at, slots[b]), 0
                    else:
                        col = b * E
                    terms = [(a[:, b * S:(b + 1) * S], w) for a, w in zip(stationary, weights)]
                    for k, (a, w) in enumerate(terms):
                        if written and b == 0:
                            name, fills = f"proj{k % 2}", len(terms) // 2
                            pe.wait_ge(taken[name], at.emptied(name, counts[name] - fills + k // 2 + 1))
                        ins = pe.matmul(bank[0:S, col:col + E], a, w, start=k == 0, stop=k == len(terms) - 1)
                    if b >= NB - len(slots):
                        done(ins, slots[b - NB + len(slots)])

            pe.wait_ge(setup_done, 1)
            with pe.Fori(0, ROUNDS) as i:
                at = Place(FRONT_LOOP, i)
                pe.wait_ge(x_loaded, (i + 1) * (32 * NU))
                for n in range(3):
                    before = at.n.get("proj1", 0)
                    pe.wait_ge(front_loaded[n], 16 * FRONT_DMAS[n])
                    for u in range(NU):
                        if n == 1:
                            pe.wait_ge(taken["proj1"], at.emptied("proj1", before - NU + u + 1))
                        if n == 2:
                            pe.wait_ge(tn_ready, at.at("tn", u + 1))
                        transposes_of(at, ftw[u])
                    pe.wait_ge(taken["proj0"], at.emptied("proj0", at.n["proj0"]))
                    start = {f"proj{e}": at.n.get(f"proj{e}", 0) for e in range(EK)}

                    def front_query(u):
                        for e in range(EK):
                            project(at, f"proj{e}", [fwq[n][:, k, e * P:(e + 1) * P] for k in range(EK)],
                                    [ftnT[u][:, k, :] for k in range(EK)])

                    def front_keys(u):
                        for b in range(NB):
                            for e in range(EK):
                                project(at, f"proj{e}", [fwk[n][:, e * P:(e + 1) * P]],
                                        [ctxT[:, ds((i * NU + u) * (NB * S2) + b * S2, S2)]])

                    def front_scores(u):
                        for b in range(NB):
                            for name in start:
                                pe.wait_ge(taken[name], at.emptied(name, start[name] + (1 + NB) * u + 2 + b))
                            name = f"score{b}"
                            k = (n * NU + u) * NB + b
                            if k >= NB:
                                if (k - NB) // (NU * NB) == 1:
                                    pe.wait_ge(exp_ready, at.at("exp", k - NB + 1))
                                else:
                                    pe.wait_ge(negmax_ready, at.at("negmax", k - NB + 1))
                            if n != 1:
                                project(at, name, [fqT[u][:, e, b * S:(b + 1) * S] for e in range(EK)],
                                        [fkT[u][:, b, e, :] for e in range(EK)])
                            else:
                                bank = banks[name]
                                for j in range(KJ):
                                    for e in range(EK):
                                        ins = pe.matmul(bank[0:KR, j * S:(j + 1) * S], fkT[u][:, b, e, j * KR:(j + 1) * KR],
                                                        fqT[u][:, e, b * S:(b + 1) * S], start=e == 0, stop=e == EK - 1)
                                done(ins, name)

                    front_query(0)
                    front_keys(0)
                    front_query(1)
                    front_scores(0)
                    front_keys(1)
                    front_scores(1)
                    before = dict(at.n)
                    if n != 1:
                        for u in range(NU):
                            for b in range(NB):
                                name = f"tr{b}"
                                pe.wait_ge(prob_ready, at.at("prob", (n * NU + u) * NB + b + 1))
                                bank = fill(at, name)
                                for j in range(KJ):
                                    ins = pe.transpose(bank[0:KR, j * S:(j + 1) * S],
                                                       prob[0:S, NB * u + b, j * KR:(j + 1) * KR], ident[0:S, 0:S])
                                done(ins, name)
                    if n == 0:
                        pe.wait_ge(ctx_loaded, (i + 1) * (16 * NU))
                    if n == 1:
                        pe.wait_ge(rows_loaded, 16 * ROW_DMAS)
                    for u in range(NU):
                        for b in range(NB):
                            if n != 1:
                                pe.wait_ge(taken[f"tr{b}"], at.emptied(f"tr{b}", before.get(f"tr{b}", 0) + u + 1))
                            else:
                                pe.wait_ge(prob_ready, at.at("prob", (n * NU + u) * NB + b + 1))
                            project(at, f"sum{b}", [fctxN[u][:, b, j, :] for j in range(KJ)],
                                    [probT[:, b, j, u * S:(u + 1) * S] for j in range(KJ)])
                    for u in range(NU):
                        for b in range(NB):
                            pe.wait_ge(taken[f"sum{b}"], at.emptied(f"sum{b}", before.get(f"sum{b}", 0) + u + 1))
                        if n != 1:
                            for e in range(EK):
                                project(at, f"proj{e}", [fwv[n][:, e * P:(e + 1) * P]], [fcT[u][:, :]])
                        else:
                            bank = fill(at, "proj1")
                            for b in range(NB):
                                o = bank[0:S, b * E:(b + 1) * E]
                                pe.matmul(o, fcT[u][:, b * S:(b + 1) * S], fwv[n], start=True, stop=False)
                                for j in range(KJ):
                                    ins = pe.matmul(o, probT[:, b, j, u * S:(u + 1) * S], fbias[0:KR, 2, :], start=False,
                                                    stop=j == KJ - 1)
                            done(ins, "proj1")
                    if n != 1:
                        for u in range(NU):
                            pe.wait_ge(taken["proj0"], at.emptied("proj0", before["proj0"] + u + 1))
                            out_rows(at, [faT[u][:, e, :] for e in range(EK)], [fwo[n][:, e, :] for e in range(EK)])
                at.check()
            pe.wait_ge(front_done, PAIRS)

            def normed(at, n, name):
                pe.wait_ge(tn_ready, at.at("tn", NB * (n + 1)))
                transposes_of(at, tn, name)

            def projected(at, name, w, m, c):
                project(at, name, [w[:, k, c * P:(c + 1) * P] for k in range(EK)], [m[:, k, :] for k in range(EK)])

            def chunked(at, w, m, chunks):
                for c in chunks:
                    projected(at, f"proj{c % 2}", w, m, c)

            def emptied(at, *names):
                for name in names:
                    pe.wait_ge(taken[name], at.emptied(name, at.n[name]))

            def values(at, banks_of_values):
                for i in banks_of_values:
                    b, n = i // V2, i % V2
                    col = HDIM + n * 512
                    project(at, f"proj{n % 2}", [tnT_next[:, k, b * S:(b + 1) * S] for k in range(EK)],
                            [w_kv[:, k, col:col + 512] for k in range(EK)])

            OUT_SLOTS = ("sum1", "proj1")

            def self_scores(at, t):
                b, c = t // GB, t % GB * 2
                if t < 2:
                    pe.wait_ge(negmax_ready, at.base("negmax"))
                else:
                    pe.wait_ge(exp_ready, at.at("exp", t - 1))
                bank = banks[f"score{t % 2}"]
                for n in range(2):
                    ins = pe.matmul(bank[0:S, n * T2:(n + 1) * T2], qT[:, c + n, b * S:(b + 1) * S],
                                    k_diag[:, c + n, :, b * S:(b + 1) * S], start=True, stop=True)
                done(ins, f"score{t % 2}")

            at = Place(START)
            normed(at, 0, "proj0")
            emptied(at, "proj0")
            pe.wait_ge(loaded["w_kv"], 16)
            values(at, range(NB * V2))
            pe.wait_ge(loaded["w_q"], 16)
            chunked(at, w_q, tnT_next, range(HC))
            chunked(at, w_kv, tnT_next, range(HC))
            at.check()
            emptied(at, "proj0", "proj1")
            for t in range(EARLY):
                self_scores(Place(MAIN_LOOP), t)

            with pe.Fori(0, L) as l:
                with pe.Fori(0, PAIRS) as p:
                    it = l * PAIRS + p
                    next_layer = (it + 1) // PAIRS
                    at = Place(MAIN_LOOP, it)

                    def weights(name):
                        pe.wait_ge(loaded[name], (l + 1) * 16)

                    for n in range(2):
                        pe.wait_ge(taken[f"proj{n}"], at.emptied(f"proj{n}", 0))
                    for t in range(SA_LAG, SG + SA_LAG + SUM_LAG):
                        if EARLY <= t < SG:
                            self_scores(at, t)
                        if 0 <= t - SA_LAG - SUM_LAG < SG:
                            g = t - SA_LAG - SUM_LAG
                            b, c = g // GB, g % GB * 2
                            pe.wait_ge(taken[f"tr{g % 2}"], at.emptied(f"tr{g % 2}", g // 2 + 1))
                            bank = fill(at, f"sum{g % 2}")
                            for n in range(2):
                                ins = pe.matmul(bank[:, n * T2:(n + 1) * T2], v[:, b, (c + n) * P:(c + n + 1) * P],
                                                probT[0:S, g % 2, 0, n * T2:(n + 1) * T2], start=True, stop=True)
                            done(ins, f"sum{g % 2}")
                        if 0 <= t - SA_LAG < SG:
                            g = t - SA_LAG
                            pe.wait_ge(prob_ready, at.at("prob", g + 1))
                            bank = fill(at, f"tr{g % 2}")
                            for h in range(G):
                                ins = pe.transpose(bank[0:S, h * S:(h + 1) * S], prob[0:S, g % PROBS, h * S:(h + 1) * S],
                                                   ident[0:S, 0:S])
                            done(ins, f"tr{g % 2}")
                    emptied(at, "sum0", "sum1")
                    normed(at, 0, "proj0")
                    weights("w_o")
                    out_rows(at, [oT[:, c, :] for c in range(HC)], [w_o[:, c, :] for c in range(HC)], slots=OUT_SLOTS)
                    emptied(at, "proj0")
                    pe.wait_ge(loaded["w_kv"], (next_layer + 1) * 16)
                    values(at, range(NB * V2 - 1))

                    normed(at, 1, "sum0")
                    values(at, range(NB * V2 - 1, NB * V2))
                    weights("c_q")
                    emptied(at, "sum0")
                    weights("c_kT")
                    for n in range(HC + 2):
                        if n < HC:
                            projected(at, f"sum{n % 2}", c_q, tnT, n)
                        if n >= 2:
                            c = n - 2
                            slot = f"sum{c % 2}"
                            pe.wait_ge(taken[slot], at.emptied(slot, (SUM_Q + c) // 2 + 1))
                            project(at, f"proj{c % 2}", [c_kT[:, c, :]], [q_diag[:, c, :, :].rearrange("p h t -> p (h t)")])
                    fills = dict(at.n)
                    pe.wait_ge(ctx_loaded, (it + PAIRS + 1) * 16)
                    pe.wait_ge(split_ready, it + 1)
                    for t in range(NH + CA_LAG + SUM_LAG):
                        if t < NH:
                            b, h = t // H, t % H
                            if b == 0 and h % 2 == 0:
                                name = f"proj{h // 2 % 2}"
                                pe.wait_ge(taken[name], at.emptied(name, fills[name] - HC // 2 + h // 4 + 1))
                            if t < 2:
                                pe.wait_ge(exp_ready, at.at("exp", SG))
                            else:
                                pe.wait_ge(negmax_ready, at.at("negmax", SG + t - 1))
                            high, low = (a[:, h, b * S:(b + 1) * S] for a in (qc_high, qc_low))
                            project(at, f"score{t % 2}", [high, high, low], [ctx_parts[:, n, b, :] for n in (0, 1, 0)])
                        if t in KEY_STEPS:
                            c = KEY_STEPS[t]
                            projected(at, f"proj{c % 2}", w_kv, tnT_next, c)
                        if 0 <= t - CA_LAG < NH:
                            i = t - CA_LAG
                            pe.wait_ge(prob_ready, at.at("prob", SG + i + 1))
                            bank = fill(at, f"tr{i % 2}")
                            for j in range(KJ):
                                ins = pe.transpose(bank[0:KR, j * S:(j + 1) * S], prob[0:S, i % PROBS, j * KR:(j + 1) * KR],
                                                   ident[0:S, 0:S])
                            done(ins, f"tr{i % 2}")
                        if 0 <= t - CA_LAG - SUM_LAG < NH and (t - CA_LAG - SUM_LAG) % G == G - 1:
                            g = (t - CA_LAG - SUM_LAG) // G
                            b = g // GB
                            for i in range(2):
                                pe.wait_ge(taken[f"tr{i}"], at.emptied(f"tr{i}", (SG + G * (g + 1)) // 2))
                            project(at, f"sum{g % 2}", [ctxN[:, b, j, :] for j in range(KJ)],
                                    [probT[:, g % 2, j, :] for j in range(KJ)])
                    weights("c_v")
                    for c in range(HC):
                        if c % 2 == 0:
                            g = SUM_CA + GB + c // 2
                            pe.wait_ge(taken[f"sum{g % 2}"], at.emptied(f"sum{g % 2}", g // 2 + 1))
                        bank = fill(at, f"proj{c % 2}")
                        for n in range(2):
                            h = 2 * c + n
                            ins = pe.matmul(bank[n * D:(n + 1) * D, 0:T2], c_v[:, h * D:(h + 1) * D], cT[:, h, :],
                                            start=True, stop=True)
                        done(ins, f"proj{c % 2}")
                    weights("c_o")
                    out_rows(at, [oT[:, c, :] for c in range(HC)], [c_o[:, c, :] for c in range(HC)], written=True,
                             slots=OUT_SLOTS)
                    pe.wait_ge(loaded["w_q"], (next_layer + 1) * 16)
                    chunked(at, w_q, tnT_next, range(HC - 1))

                    normed(at, 2, "sum0")
                    chunked(at, w_q, tnT_next, range(HC - 1, HC))
                    fills = dict(at.n)
                    weights("f_1")
                    emptied(at, "sum0")
                    chunked(at, f_1, tnT, range(FC))
                    for name in ("proj0", "proj1"):
                        pe.wait_ge(taken[name], at.emptied(name, fills[name]))
                    for t in range(EARLY - 2):
                        self_scores(Place(MAIN_LOOP, it + 1), t)
                    weights("f_2")
                    out_rows(at, [hT[:, c, :] for c in range(FC)], [f_2[:, c, :] for c in range(FC)], written=True,
                             slots=OUT_SLOTS, between=lambda: self_scores(Place(MAIN_LOOP, it + 1), EARLY - 2))
                    self_scores(Place(MAIN_LOOP, it + 1), EARLY - 1)
                    at.check()

        @block.scalar
        def _(act):
            def filled(at, name):
                act.wait_ge(ready[name], at.at(name, at.next(name) + 1))
                return banks[name]

            def copy(o, i):
                return act.activation(o, i, ACT.Copy)

            def plus(o, i, bias):
                return act.activation(o, i, ACT.Identity, bias=bias)

            def softmax_row(at, k, o, i, scale, col):
                act.wait_ge(negmax_ready, at.at("negmax", k + 1))
                act.activation(o, i, ACT.Exp, bias=negmax[0:S, col:col + 1], scale=scale,
                               accum_out=total[0:S, col:col + 1]).then_inc(exp_ready, 1)

            act.wait_ge(setup_done, 1)
            with act.Fori(0, ROUNDS) as i:
                at = Place(FRONT_LOOP, i)
                for n in range(3):
                    def front_query(u):
                        bank = filled(at, "proj0")
                        plus(fqT[u][:, 0, :], bank[:, 0:T2], fcol[:, n, 0, 0:1]).then_inc(taken["proj0"], 1)

                    def front_keys(u):
                        for b in range(NB):
                            bank = filled(at, "proj0")
                            plus(fkT[u][:, b, 0, :], bank[:, 0:S2], fcol[:, n, 1, 0:1]).then_inc(taken["proj0"], 1)

                    def front_softmax(u):
                        for b in range(NB):
                            m, k = NB * u + b, (n * NU + u) * NB + b
                            if n != 1:
                                softmax_row(at, k, prob[0:S, m, 0:S2], prob[0:S, m, 0:S2], -1.0, m)
                            else:
                                bank = banks[f"score{b}"]
                                act.wait_ge(negmax_ready, at.at("negmax", k + 1))
                                for j in range(KJ):
                                    col = NU * NB + KJ * m + j
                                    ins = act.activation(prob[0:KR, m, j * S:(j + 1) * S], bank[0:KR, j * S:(j + 1) * S],
                                                         ACT.Exp, bias=negmax[0:KR, col:col + 1], scale=FRONT_SCALE,
                                                         accum_out=total[0:KR, col:col + 1])
                                ins.then_inc(exp_ready, 1)

                    act.wait_ge(front_loaded[n], 16 * FRONT_DMAS[n])
                    for u in range(NU):
                        bank = filled(at, "proj0")
                        copy(ftnT[u][:, :, :].rearrange("p k t -> p (k t)"), bank[:, 0:EK * T2]).then_inc(taken["proj0"], 1)
                    front_query(0)
                    front_keys(0)
                    front_query(1)
                    front_softmax(0)
                    front_keys(1)
                    front_softmax(1)
                    if n != 1:
                        for u in range(NU):
                            bank = filled(at, "tr0")
                            copy(probT[:, 0, :, u * S:(u + 1) * S], bank[0:KR, 0:KJ * S].rearrange("p (j s) -> p j s", j=KJ))\
                                .then_inc(taken["tr0"], 1)
                    for u in range(NU):
                        bank = filled(at, "sum0")
                        copy(fcT[u][:, 0:S], bank[:, 0:S]).then_inc(taken["sum0"], 1)
                    if n != 1:
                        for u in range(NU):
                            bank = filled(at, "proj0")
                            plus(faT[u][:, 0, :], bank[:, 0:T2], fcol[:, n, 2, 0:1]).then_inc(taken["proj0"], 1)

            def normed(at, o, scale_bias, name):
                bank = filled(at, name)
                for k in range(EK):
                    ins = act.activation(o[:, k, :], bank[:, k * T2:(k + 1) * T2], ACT.Identity,
                                         scale=scale_bias[:, 0, k:k + 1], bias=scale_bias[:, 1, k:k + 1])
                ins.then_inc(taken[name], 1)

            def self_exponentials(at, t):
                if t >= PROBS:
                    act.wait_ge(ready[f"tr{t % 2}"], at.at(f"tr{t % 2}", (t - PROBS) // 2 + 1))
                act.wait_ge(negmax_ready, at.at("negmax", t + 1))
                bank = banks[f"score{t % 2}"]
                for h in range(G):
                    col = G * t + h
                    ins = act.activation(prob[0:S, t % PROBS, h * S:(h + 1) * S], bank[0:S, h * S:(h + 1) * S],
                                         ACT.Exp, bias=negmax[0:S, col:col + 1], scale=SCALE,
                                         accum_out=total[0:S, col:col + 1])
                ins.then_inc(exp_ready, 1)

            def diagonal(at, name, o, c):
                bank = filled(at, name)
                for h in range(2):
                    ins = copy(o[h * D:(h + 1) * D, c, h, :], bank[h * D:(h + 1) * D, 0:T2])
                ins.then_inc(taken[name], 1)

            def chunk(at, o, n, func=ACT.Copy, **kw):
                bank = filled(at, "proj0")
                act.activation(o, bank[0:o.shape[0], 0:n], func, **kw).then_inc(taken["proj0"], 1)

            def values(at):
                for b in range(NB):
                    chunk(at, v[:, b, 0:512], 512)

            def queries(at):
                for c in range(0, HC, 2):
                    chunk(at, qT[:, c, :], T2)

            at = Place(START)
            act.wait_ge(rows_loaded, 16 * ROW_DMAS)
            normed(at, tnT_next, norm, "proj0")
            values(at)
            queries(at)
            for c in range(0, HC, 2):
                diagonal(at, "proj0", k_diag, c)
            at.check()
            for t in range(EARLY):
                self_exponentials(Place(MAIN_LOOP), t)
            with act.Fori(0, L) as l:
                with act.Fori(0, PAIRS) as p:
                    at = Place(MAIN_LOOP, l * PAIRS + p)

                    for t in range(SA_LAG, SG + SA_LAG + SUM_LAG):
                        if 0 <= t - SA_LAG - SUM_LAG < SG and (t - SA_LAG - SUM_LAG) % 2 == 0:
                            b, c = (t - SA_LAG - SUM_LAG) // GB, (t - SA_LAG - SUM_LAG) % GB * 2
                            bank = filled(at, "sum0")
                            for h in range(2):
                                r = slice(h * D, (h + 1) * D)
                                ins = copy(oT[r, c:c + 2, b * S:(b + 1) * S],
                                           bank[r, 0:2 * T2].rearrange("p (n h s) -> p n h s", n=2, h=2)[:, :, h, :])
                            ins.then_inc(taken["sum0"], 1)
                        if 0 <= t - SA_LAG < SG and (t - SA_LAG) % 2 == 0:
                            bank = filled(at, "tr0")
                            copy(probT[0:S, 0, 0, :], bank[0:S, 0:G * S]).then_inc(taken["tr0"], 1)
                        if EARLY <= t < SG:
                            self_exponentials(at, t)

                    normed(at, tnT_next, norm, "proj0")
                    values(at)
                    normed(at, tnT, norm, "sum0")
                    def upper_part(c):
                        name = f"proj{c % 2}"
                        act.wait_ge(ready[name], at.at(name, KT + c // 2 + 1))
                        copy(qc_high[:, 2 * c:2 * c + 2, :].rearrange("p h t -> p (h t)"), banks[name][:, 0:2 * T2])\
                            .then_inc(high_ready, 1)

                    for n in range(0, HC + 4, 2):
                        if 0 <= n - 3:
                            upper_part(n - 3)
                        if n < HC:
                            diagonal(at, "sum0", q_diag, n)
                        if 0 <= n - 2 < HC:
                            upper_part(n - 2)
                    at.n["proj0"] += HC // 2
                    for t in range(NH + CA_LAG + SUM_LAG):
                        if 0 <= t - CA_LAG < NH and (t - CA_LAG) % 2 == 0:
                            i = t - CA_LAG
                            if i % G == 0:
                                g = SUM_CA + i // G
                                act.wait_ge(ready[f"sum{g % 2}"], at.at(f"sum{g % 2}", g // 2))
                            bank = filled(at, "tr0")
                            copy(probT[:, i // G % 2, :, i % G * S:(i % G + 1) * S],
                                 bank[0:KR, 0:KJ * S].rearrange("p (j s) -> p j s", j=KJ)).then_inc(taken["tr0"], 1)
                        if t < NH:
                            k = SG + t
                            row = prob[0:S, t % PROBS, 0:S2]
                            softmax_row(at, k, row, row, -1.0, G * SG + t)
                        if 0 <= t - CA_LAG - SUM_LAG < NH and (t - CA_LAG - SUM_LAG) % (2 * G) == G - 1:
                            g = (t - CA_LAG - SUM_LAG) // G
                            b, h = g // GB, g % GB * G
                            bank = filled(at, "sum0")
                            copy(cT[:, h:h + G, b * S:(b + 1) * S], bank[:, 0:G * S].rearrange("p (h s) -> p h s", h=G))\
                                .then_inc(taken["sum0"], 1)
                        if KEY_STEPS.get(t, 1) % 2 == 0:
                            diagonal(at, "proj0", k_diag, KEY_STEPS[t])
                    for c in range(0, HC, 2):
                        chunk(at, oT[:, c, :], T2)
                    queries(at)
                    act.wait_ge(loaded["small"], (l + 1) * (16 * SMALL))
                    normed(at, tnT, pre, "sum0")
                    early = Place(MAIN_LOOP, l * PAIRS + p + 1)
                    for c in range(0, FC, 2):
                        chunk(at, hT[:, c, :], T2, ACT.Relu, bias=f_b1[:, c:c + 1])
                    for t in range(EARLY):
                        self_exponentials(early, t)
                    assert at.n["proj0"] == MAIN["proj0"] and at.n["tr0"] == MAIN["tr0"] and at.n["sum0"] == MAIN["sum0"]

        @block.vector
        def _(dve):
            def filled(at, name):
                dve.wait_ge(ready[name], at.at(name, at.next(name) + 1))
                return banks[name]

            def gate(s, value):
                dve.wait_ge(s, value)
                dve.sem_inc(passed, 1)

            def link(at, ins):
                ins.then_inc(dve_step, 1)
                linked(at)

            def linked(at):
                gate(dve_step, at.at("dve", at.next("dve") + 1))

            def plus(o, i, bias):
                return dve.tensor_scalar(o, i, bias, None, ALU.add)

            def statistics(at, a, u=0):
                for b in range(NB):
                    ins = dve.bn_stats(stats[:, b, :], a[:, b, :])
                variances(at, ins, u)

            def variances(at, ins, u=0):
                link(at, ins)
                for b in range(NB):
                    ins = dve.bn_aggr(mv2[:, u, b, :], stats[:, b, :])
                ins.then_inc(stats_ready, 1)

            def wait_rstd(at):
                dve.wait_ge(rstd_ready, at.at("stats", at.next("stats") + 1))

            def normalise(o, a, b, u=0):
                return dve.tensor_scalar(o, a[:, b, :], mv2[:, u, b, 0:1], rstd2[:, u, b:b + 1], ALU.subtract, ALU.mult)

            dve.wait_ge(setup_done, 1)
            with dve.Fori(0, ROUNDS) as i:
                at = Place(FRONT_LOOP, i)
                dve.wait_ge(x_loaded, (i + 1) * (32 * NU))
                for n in range(3):
                    def front_query(u):
                        bank = filled(at, "proj1")
                        plus(fqT[u][:, 1, :], bank[:, 0:T2], fcol[:, n, 0, 1:2]).then_inc(taken["proj1"], 1)

                    def front_keys(u):
                        for b in range(NB):
                            bank = filled(at, "proj1")
                            plus(fkT[u][:, b, 1, :], bank[:, 0:S2], fcol[:, n, 1, 1:2]).then_inc(taken["proj1"], 1)

                    def columns_of(m):
                        return slice(NU * NB + KJ * m, NU * NB + KJ * (m + 1))

                    def front_maxima(u):
                        for b in range(NB):
                            m = NB * u + b
                            if n != 1:
                                k = at.next(f"score{b}")
                                gate(ready[f"score{b}"], at.at(f"score{b}", k + 1))
                                dve.tensor_tensor_reduce(out=prob[0:S, m, 0:S2], in0=banks[f"score{b}"][0:S, 0:S2], in1=cbias[:, b, :],
                                                         scale=-FRONT_SCALE, scalar=3.4e38, op0=ALU.add, op1=ALU.min,
                                                         accum_out=negmax[0:S, m:m + 1]).then_inc(negmax_ready, 1)
                            else:
                                bank = filled(at, f"score{b}")
                                link(at, dve.reduce_max(rtotal[0:KR, columns_of(m)],
                                                        bank[0:KR, 0:KJ * S].rearrange("p (j s) -> p j s", j=KJ), AX.X))
                                dve.tensor_scalar(negmax[0:KR, columns_of(m)], rtotal[0:KR, columns_of(m)], -FRONT_SCALE,
                                                  None, ALU.mult).then_inc(negmax_ready, 1)

                    def front_probabilities(u):
                        for b in range(NB):
                            m = NB * u + b
                            dve.wait_ge(exp_ready, at.at("exp", (n * NU + u) * NB + b + 1))
                            if n != 1:
                                link(at, dve.reciprocal(rtotal[0:S, m:m + 1], total[0:S, m:m + 1]))
                                dve.tensor_scalar(prob[0:S, m, 0:S2], prob[0:S, m, 0:S2], rtotal[0:S, m:m + 1], None,
                                                  ALU.mult).then_inc(prob_ready, 1)
                            else:
                                link(at, dve.reciprocal(rtotal[0:KR, columns_of(m)], total[0:KR, columns_of(m)]))
                                dve.tensor_tensor(probT[:, b, :, u * S:(u + 1) * S],
                                                  prob[0:KR, m, 0:KJ * S].rearrange("p (j s) -> p j s", j=KJ),
                                                  rtotal[0:KR, columns_of(m)].unsqueeze(2).broadcast_to([KR, KJ, S]), ALU.mult)\
                                    .then_inc(prob_ready, 1)

                    dve.wait_ge(front_loaded[n], 16 * FRONT_DMAS[n])
                    if n == 1:
                        dve.wait_ge(rows_loaded, 16 * ROW_DMAS)
                    front_query(0)
                    front_keys(0)
                    front_query(1)
                    front_maxima(0)
                    front_keys(1)
                    front_probabilities(0)
                    front_maxima(1)
                    front_probabilities(1)
                    if n != 1:
                        for u in range(NU):
                            bank = filled(at, "tr1")
                            dve.tensor_copy(probT[:, 1, :, u * S:(u + 1) * S],
                                            bank[0:KR, 0:KJ * S].rearrange("p (j s) -> p j s", j=KJ)).then_inc(taken["tr1"], 1)
                    for u in range(NU):
                        bank = filled(at, "sum1")
                        dve.tensor_copy(fcT[u][:, S:T2], bank[:, 0:S]).then_inc(taken["sum1"], 1)
                    if n != 1:
                        for u in range(NU):
                            bank = filled(at, "proj1")
                            plus(faT[u][:, 1, :], bank[:, 0:T2], fcol[:, n, 2, 1:2]).then_inc(taken["proj1"], 1)
                    for u in range(NU):
                        if n != 1:
                            dve.wait_ge(resid_ready, at.at("resid", at.next("resid") + 1))
                        bank = filled(at, "proj1")
                        dve.tensor_tensor(ftw[u][:, :, :], bank[0:S, 0:NB * E].rearrange("p (b e) -> p b e", b=NB),
                                          ftw[u][:, :, :], ALU.add).then_inc(taken["proj1"], 1)
                        if n == 1:
                            dve.wait_ge(taken["proj1"], at.emptied("proj1", at.n["proj1"]))
                            statistics(at, ftw[u], u)
                    if n == 1:
                        for u in range(NU):
                            wait_rstd(at)
                            for b in range(NB):
                                ins = normalise(ftn[u][:, b, :], ftw[u], b, u)
                            link(at, ins)
                            link(at, dve.tensor_tensor(ftn[u][:, :, :], ftn[u][:, :, :],
                                                       fbias[0:S, 3, :].unsqueeze(1).broadcast_to([S, NB, E]), ALU.mult))
                            dve.tensor_tensor(ftw[u][:, :, :], ftn[u][:, :, :],
                                              fbias[0:S, 4, :].unsqueeze(1).broadcast_to([S, NB, E]), ALU.add)\
                                .then_inc(tn_ready, 1)
                for u in range(NU):
                    dve.wait_ge(taken["proj1"], at.emptied("proj1", at.n["proj1"] - NU + u + 1))
                    dve.tensor_copy(t_all[:, ds((i * NU + u) * NB, NB), :], ftw[u][:, :, :])
                    pair_ctx = ctxT[:, ds((i * NU + u) * (NB * S2), NB * S2)]
                    dve.scalar_tensor_tensor(pair_ctx, fcmask[u].rearrange("p b s -> p (b s)"), 0.0, pair_ctx,
                                             ALU.not_equal, ALU.mult).then_inc(front_done, 1)

            dve.wait_ge(front_done, PAIRS)

            def normed(at, a):
                wait_rstd(at)
                for b in range(NB):
                    normalise(tn[:, b, :], a, b).then_inc(tn_ready, 1)

            def diagonal(at, name, o, c):
                bank = filled(at, name)
                for h in range(2):
                    ins = dve.tensor_copy(o[h * D:(h + 1) * D, c, h, :], bank[h * D:(h + 1) * D, 0:T2])
                ins.then_inc(taken[name], 1)

            def chunk(at, o, n):
                bank = filled(at, "proj1")
                dve.tensor_copy(o, bank[0:o.shape[0], 0:n]).then_inc(taken["proj1"], 1)

            def values(at, b):
                chunk(at, v[:, b, 512:1024], 512)

            def new_smask(it):
                dve.wait_ge(smask_loaded, (it + 1) * 16)
                dve.tensor_scalar(smask0[:, :, :], smask[:, :, :], 0.0, None, ALU.is_equal).then_inc(smask_used, 1)
                gate(smask_used, it + 1)

            def self_reciprocals(at, t):
                cols = slice(G * t, G * t + G)
                dve.wait_ge(exp_ready, at.at("exp", t + 1))
                dve.reciprocal(rtotal[0:S, cols], total[0:S, cols]).then_inc(rtotal_ready, 1)

            def queries(at, chunks):
                for c in chunks:
                    chunk(at, qT[:, c, :], T2)

            def self_maxima(at, t, here, meanwhile=None):
                name = f"score{t % 2}"
                b, cols = t // GB, slice(G * t, G * t + G)
                gate(ready[name], at.at(name, t // 2 + 1))
                four = banks[name][0:S, 0:G * S].rearrange("p (h k) -> p h k", h=G)
                dve.copy_predicated(four, smask0[:, b, :].unsqueeze(1).broadcast_to([S, G, S]),
                                    masked[:, 0:1].unsqueeze(1).broadcast_to([S, G, S])).then_inc(dve_step, 1)
                if meanwhile:
                    meanwhile()
                linked(here)
                dve.reduce_max(rtotal[0:S, cols], four, AX.X).then_inc(dve_step, 1)
                if t > 0:
                    self_reciprocals(at, t - 1)
                linked(here)
                dve.tensor_scalar(negmax[0:S, cols], rtotal[0:S, cols], -SCALE, None, ALU.mult).then_inc(negmax_ready, 1)

            at = Place(START)
            new_smask(0)
            first = t_all[:, 0:NB, :]
            statistics(at, first)
            normed(at, first)
            for b in range(NB):
                values(at, b)
            queries(at, range(1, HC, 2))
            for c in range(1, HC, 2):
                diagonal(at, "proj1", k_diag, c)
            for t in range(EARLY):
                self_maxima(Place(MAIN_LOOP), t, at)
            at.check()
            with dve.Fori(0, L) as l:
                with dve.Fori(0, PAIRS) as p:
                    it = l * PAIRS + p
                    at = Place(MAIN_LOOP, it)
                    next_tokens = t_all[:, ds((p + 1) % PAIRS * NB, NB), :]

                    def residual(o, with_statistics=True, between=None):
                        dve.wait_ge(resid_ready, at.at("resid", at.next("resid") + 1))
                        for b, name in enumerate(("sum1", "proj1")):
                            if between and b == 1:
                                between()
                            bank = filled(at, name)
                            dve.tensor_tensor(o[:, b, :], bank[0:S, 0:E], tw[:, b, :], ALU.add).then_inc(taken[name], 1)
                            if with_statistics:
                                dve.wait_ge(taken[name], at.emptied(name, at.n[name]))
                                ins = dve.bn_stats(stats[:, b, :], o[:, b, :])
                        if with_statistics:
                            variances(at, ins)

                    for t in range(SA_LAG, SG + SA_LAG + SUM_LAG):
                        def empty_sum1():
                            g = t - SA_LAG - SUM_LAG
                            if 0 <= g < SG and g % 2 == 1:
                                b, c = g // GB, g % GB * 2
                                bank = filled(at, "sum1")
                                for h in range(2):
                                    r = slice(h * D, (h + 1) * D)
                                    ins = dve.tensor_copy(oT[r, c:c + 2, b * S:(b + 1) * S],
                                                          bank[r, 0:2 * T2].rearrange("p (n h s) -> p n h s", n=2, h=2)[:, :, h, :])
                                ins.then_inc(taken["sum1"], 1)

                        if EARLY <= t < SG:
                            self_maxima(at, t, at, meanwhile=empty_sum1)
                        else:
                            empty_sum1()
                        if 0 <= t - SA_LAG < SG and (t - SA_LAG) % 2 == 1:
                            bank = filled(at, "tr1")
                            dve.tensor_copy(probT[0:S, 1, 0, :], bank[0:S, 0:G * S]).then_inc(taken["tr1"], 1)
                        if t == SG:
                            self_reciprocals(at, SG - 1)
                            statistics(at, next_tokens)
                        if t == SG + 2:
                            normed(at, next_tokens)
                    dve.wait_ge(cmask_loaded, (it + 1) * 16)
                    dve.tensor_scalar(cbias[:, :, :], cmask[0:S, :, :], 0.0, MASKED, ALU.is_equal, ALU.mult)\
                        .then_inc(cbias_written, 1)
                    gate(cbias_written, it + 1)
                    residual(tw)
                    values(at, 0)
                    normed(at, tw)
                    values(at, 1)
                    def lower_part(c):
                        name = f"proj{c % 2}"
                        columns = slice(2 * c, 2 * c + 2)
                        dve.wait_ge(high_ready, at.at("high", c + 1))
                        dve.tensor_tensor(qc_low[:, columns, :].rearrange("p h t -> p (h t)"), banks[name][:, 0:2 * T2],
                                          qc_high[:, columns, :].rearrange("p h t -> p (h t)").bitcast(f32), ALU.subtract)\
                            .then_inc(taken[name], 1)

                    for n in range(1, HC + 2, 2):
                        if n >= 3:
                            lower_part(n - 3)
                        if n < HC:
                            diagonal(at, "sum1", q_diag, n)
                        if n >= 3:
                            lower_part(n - 2)
                    at.n["proj1"] += HC // 2
                    for t in range(NH + CA_LAG + SUM_LAG):
                        if t < NH:
                            name = f"score{t % 2}"
                            col = G * SG + t
                            if t >= PROBS:
                                gate(ready[f"tr{t % 2}"], at.at(f"tr{t % 2}", (SG + t - PROBS) // 2 + 1))
                            gate(ready[name], at.at(name, (SG + t) // 2 + 1))
                            dve.tensor_tensor_reduce(out=prob[0:S, t % PROBS, 0:S2], in0=banks[name][0:S, 0:S2],
                                                     in1=cbias[:, t // H, :], scale=-SCALE, scalar=3.4e38,
                                                     op0=ALU.add, op1=ALU.min, accum_out=negmax[0:S, col:col + 1])\
                                .then_inc(negmax_ready, 1)
                        if 0 <= t - 1 < NH:
                            col = G * SG + t - 1
                            dve.wait_ge(exp_ready, at.at("exp", SG + t))
                            dve.reciprocal(rtotal[0:S, col:col + 1], total[0:S, col:col + 1]).then_inc(rtotal_ready, 1)
                        if 0 <= t - CA_LAG < NH and (t - CA_LAG) % 2 == 1:
                            i = t - CA_LAG
                            if i % G == 1:
                                g = SUM_CA + i // G
                                dve.wait_ge(ready[f"sum{g % 2}"], at.at(f"sum{g % 2}", g // 2))
                            bank = filled(at, "tr1")
                            dve.tensor_copy(probT[:, i // G % 2, :, i % G * S:(i % G + 1) * S],
                                            bank[0:KR, 0:KJ * S].rearrange("p (j s) -> p j s", j=KJ)).then_inc(taken["tr1"], 1)
                        if 0 <= t - CA_LAG - SUM_LAG < NH and (t - CA_LAG - SUM_LAG) % (2 * G) == 2 * G - 1:
                            g = (t - CA_LAG - SUM_LAG) // G
                            b, h = g // GB, g % GB * G
                            bank = filled(at, "sum1")
                            dve.tensor_copy(cT[:, h:h + G, b * S:(b + 1) * S],
                                            bank[:, 0:G * S].rearrange("p (h s) -> p h s", h=G)).then_inc(taken["sum1"], 1)
                        if KEY_STEPS.get(t, 0) % 2 == 1:
                            diagonal(at, "proj1", k_diag, KEY_STEPS[t])
                    for c in range(1, HC, 2):
                        chunk(at, oT[:, c, :], T2)
                    residual(tw)
                    queries(at, (1,))
                    normed(at, tw)
                    queries(at, range(3, HC, 2))
                    new_smask(it + 1)
                    early = Place(MAIN_LOOP, it + 1)
                    for c in range(1, FC, 2):
                        bank = filled(at, "proj1")
                        dve.tensor_scalar(hT[:, c, :], bank[:, 0:T2], f_b1[:, c:c + 1], 0.0, ALU.add, ALU.max)\
                            .then_inc(taken["proj1"], 1)
                    for t in range(EARLY - 2):
                        self_maxima(early, t, at)
                    residual(t_all[:, ds(p * NB, NB), :], False, between=lambda: self_maxima(early, EARLY - 2, at))
                    self_maxima(early, EARLY - 1, at)
                    assert all(at.n[k] == MAIN[k] for k in ("proj1", "tr1", "sum1", "dve", "stats", "resid"))


_DECODER = ["sa_kv", "sa_q", "sa_ow", "sa_ob", "ca_kv", "ca_q", "ca_ow", "ca_ob", "ff_w1", "ff_b1", "ff_w2", "ff_b2",
            "pre_g", "pre_b", "norm_g", "norm_b"]
_COLUMNS = ("bq", "bk", "bv", "ff_b1", "pre_g", "pre_b", "norm_g", "norm_b")
_FRONT = [["Wq", "bq", "Wk", "bk", "Wv", "bv", "Wo", "bo"], ["Wq", "bq", "Wk", "bk", "Wv", "bv", "gamma", "beta"],
          ["Wq", "bq", "Wk", "bk", "Wv", "bv", "Wo", "bo"]]


def kernel(**inputs):
    import numpy as _np
    import concourse.bacc as _bacc
    from concourse import mybir as _mybir
    from concourse.bass_utils import run_bass_kernel_spmd as _run

    nc = _bacc.Bacc("TRN2", target_bir_lowering=False, num_devices=1)
    arrays = {}

    def give(name, a):
        a = _np.ascontiguousarray(a)
        arrays[name] = a
        return nc.dram_tensor(name, a.shape, _mybir.dt.from_np(a.dtype), kind="ExternalInput").ap()

    x = _np.asarray(inputs["x"])
    ctx = _np.asarray(inputs["ctx_512"])
    mask = _np.asarray(inputs["mask_Bx1xS2_if1"])
    hd = inputs["L3_xattn_sa_q"].shape[2]

    def columns(a):
        a = _np.asarray(a)
        return _np.swapaxes(a.reshape(a.shape[:-1] + (-1, 128)), -1, -2)

    dec = {n: give(n, (columns if n in _COLUMNS else _np.asarray)(inputs["L3_xattn_" + n])) for n in _DECODER}
    dec["ca_kT"] = give("ca_kT", _np.asarray(inputs["L3_xattn_ca_kv"])[:, :, 0:hd].transpose(0, 2, 1))
    front = [{n: give(f"L{i}_{n}", (columns if n in _COLUMNS else _np.asarray)(inputs[f"L{i}_xattn_{n}"])) for n in names}
             for i, names in enumerate(_FRONT)]
    front[1]["bv_row"] = give("L1_bv_row", _np.asarray(inputs["L1_xattn_bv"]))
    args = [give("x", x), give("ctx", ctx), give("ctx_T", ctx.reshape(-1, ctx.shape[2]).T),
            give("self_mask", _np.asarray(inputs["mask_BxSxS_ik0"])), give("ctx_mask", mask.reshape(mask.shape[0], -1))]
    out = nc.dram_tensor("out", x.shape, _mybir.dt.float32, kind="ExternalOutput").ap()
    attention_layers(nc, *args, front, dec, out)
    return _run(nc, [arrays], core_ids=[0]).results[0]["out"]
```
